# Optimizing a Trainium2 kernel written in Bass

```python
import numpy as np
import jax
import jax.numpy as jnp

def _softmax(x, axis=-1):
    return jax.nn.softmax(x, axis=axis)

def _gelu(x):
    return jax.nn.gelu(x, approximate=True)

def _silu(x):
    return jax.nn.silu(x)

def _sigmoid(x):
    return jax.nn.sigmoid(x)

def _layernorm(x, axis=-1, eps=1e-05):
    m = jnp.mean(x, axis=axis, keepdims=True)
    v = jnp.var(x, axis=axis, keepdims=True)
    return (x - m) / jnp.sqrt(v + eps)

def _scatter_add(tgt, idx, src, axis=0):
    return tgt.at[idx].add(src)

def _segment_sum(src, seg, n):
    return jax.ops.segment_sum(src, seg, n)
kernel_name = 'mk_adj_resnorm_d2_adj_r2_0ec048'

def setup_inputs(seed: int=0):
    np.random.seed(seed)
    _w = jnp.asarray

    def _rec_inputs():
        import jax
        import jax.numpy as jnp
        _gk = jax.random.key(seed)
        x = -0.0005207 + 1.001 * jax.random.normal(jax.random.fold_in(_gk, 1), (4096, 128), jnp.float32)
        _a = jax.random.bernoulli(jax.random.fold_in(_gk, 2), 0.00390625, (4096, 4096))
        _a = jnp.logical_or(_a, jnp.swapaxes(_a, -1, -2))
        _a = jnp.logical_or(_a, jnp.eye(4096, dtype=bool))
        _af = _a.astype(jnp.float32)
        _af = _af * jax.random.uniform(jax.random.fold_in(_gk, 3), (4096, 4096), jnp.float32, 0.05, 1)
        adj = _af
        return (x, adj)
    x, adj = _rec_inputs()

    def _L0_gnn_setup():
        import jax, jax.numpy as jnp
        import numpy as np
        N, IN_DIM, HID = (4096, 128, 128)

        def _gcn_layer(x, adj, W, b):
            d_inv_sqrt = (jnp.sum(adj, axis=1) + 1e-09) ** (-0.5)
            msg = d_inv_sqrt[:, None] * adj * d_inv_sqrt[None, :] @ x
            return jax.nn.relu(msg @ W + b)
        key = jax.random.key(seed)
        ks = jax.random.split(key, 9)
        feature_x = jax.random.normal(ks[0], (N, IN_DIM), dtype=jnp.float32)
        spatial_x = jax.random.normal(ks[1], (N, IN_DIM), dtype=jnp.float32)
        adj = jax.random.uniform(ks[2], (N, N), dtype=jnp.float32)
        s_in = 1.0 / np.sqrt(IN_DIM)
        s_hid = 1.0 / np.sqrt(2 * HID)
        W_f = jax.random.uniform(ks[3], (IN_DIM, HID), dtype=jnp.float32, minval=-s_in, maxval=s_in)
        b_f = jax.random.uniform(ks[4], (HID,), dtype=jnp.float32, minval=-s_in, maxval=s_in)
        W_s = jax.random.uniform(ks[5], (IN_DIM, HID), dtype=jnp.float32, minval=-s_in, maxval=s_in)
        b_s = jax.random.uniform(ks[6], (HID,), dtype=jnp.float32, minval=-s_in, maxval=s_in)
        W_att = jax.random.uniform(ks[7], (2 * HID, 1), dtype=jnp.float32, minval=-s_hid, maxval=s_hid)
        b_att = jax.random.uniform(ks[8], (1,), dtype=jnp.float32, minval=-s_hid, maxval=s_hid)
        return {'feature_x': feature_x, 'spatial_x': spatial_x, 'adj': adj, 'W_f': W_f, 'b_f': b_f, 'W_s': W_s, 'b_s': b_s, 'W_att': W_att, 'b_att': b_att}
    _L0_gnn_all = _L0_gnn_setup()
    _L0_gnn_in = {k: v for k, v in _L0_gnn_all.items() if k in ('spatial_x', 'W_f', 'b_f', 'W_s', 'b_s', 'W_att', 'b_att')}
    del _L0_gnn_all

    def _L1_gnn_setup():
        import jax, jax.numpy as jnp
        import numpy as np
        N = 4096
        D = 128
        L = 3

        def _cxin_conv(x, a, eps, W, b):
            ax = a @ x
            h = ax + (1.0 + eps[0]) * ax
            for i in range(L):
                h = jax.nn.relu(h @ W[i].T + b[i])
            return h
        key = jax.random.key(seed)
        ks = jax.random.split(key, 8)
        s = 1.0 / np.sqrt(D)
        return {'x1': jax.random.normal(ks[0], (N, D), jnp.float32), 'x2': jax.random.normal(ks[1], (N, D), jnp.float32), 'G1': jax.random.uniform(ks[2], (N, N), jnp.float32), 'G2': jax.random.uniform(ks[3], (N, N), jnp.float32), 'eps1': jnp.zeros((1,), jnp.float32), 'eps2': jnp.zeros((1,), jnp.float32), 'W1': jax.random.normal(ks[4], (L, D, D), jnp.float32) * s, 'b1': jnp.zeros((L, D), jnp.float32), 'W2': jax.random.normal(ks[5], (L, D, D), jnp.float32) * s, 'b2': jnp.zeros((L, D), jnp.float32), 'Wm': jax.random.normal(ks[6], (D, 2 * D), jnp.float32) * (1.0 / np.sqrt(2 * D)), 'bm': jnp.zeros((D,), jnp.float32)}
    _L1_gnn_all = _L1_gnn_setup()
    _L1_gnn_in = {k: v for k, v in _L1_gnn_all.items() if k in ('x2', 'eps1', 'eps2', 'W1', 'b1', 'W2', 'b2', 'Wm', 'bm')}
    del _L1_gnn_all
    return {'x': x, 'adj': adj, 'L0_gnn_spatial_x': _L0_gnn_in['spatial_x'], 'L0_gnn_W_f': _L0_gnn_in['W_f'], 'L0_gnn_b_f': _L0_gnn_in['b_f'], 'L0_gnn_W_s': _L0_gnn_in['W_s'], 'L0_gnn_b_s': _L0_gnn_in['b_s'], 'L0_gnn_W_att': _L0_gnn_in['W_att'], 'L0_gnn_b_att': _L0_gnn_in['b_att'], 'L1_gnn_x2': _L1_gnn_in['x2'], 'L1_gnn_eps1': _L1_gnn_in['eps1'], 'L1_gnn_eps2': _L1_gnn_in['eps2'], 'L1_gnn_W1': _L1_gnn_in['W1'], 'L1_gnn_b1': _L1_gnn_in['b1'], 'L1_gnn_W2': _L1_gnn_in['W2'], 'L1_gnn_b2': _L1_gnn_in['b2'], 'L1_gnn_Wm': _L1_gnn_in['Wm'], 'L1_gnn_bm': _L1_gnn_in['bm']}

def reference(x, adj, L0_gnn_spatial_x, L0_gnn_W_f, L0_gnn_b_f, L0_gnn_W_s, L0_gnn_b_s, L0_gnn_W_att, L0_gnn_b_att, L1_gnn_x2, L1_gnn_eps1, L1_gnn_eps2, L1_gnn_W1, L1_gnn_b1, L1_gnn_W2, L1_gnn_b2, L1_gnn_Wm, L1_gnn_bm):
    import jax
    import jax.numpy as jnp

    def _L0_gnn_ref(feature_x, spatial_x, adj, W_f, b_f, W_s, b_s, W_att, b_att):
        import jax, jax.numpy as jnp
        import numpy as np
        N, IN_DIM, HID = (4096, 128, 128)

        def _gcn_layer(x, adj, W, b):
            d_inv_sqrt = (jnp.sum(adj, axis=1) + 1e-09) ** (-0.5)
            msg = d_inv_sqrt[:, None] * adj * d_inv_sqrt[None, :] @ x
            return jax.nn.relu(msg @ W + b)
        H_f = _gcn_layer(feature_x, adj, W_f, b_f)
        H_s = _gcn_layer(spatial_x, adj, W_s, b_s)
        H_cat = jnp.concatenate([H_f, H_s], axis=1)
        attn = jax.nn.sigmoid(H_cat @ W_att + b_att)
        return attn * H_f + (1.0 - attn) * H_s

    def _L1_gnn_ref(x1, x2, G1, G2, eps1, eps2, W1, b1, W2, b2, Wm, bm):
        import jax, jax.numpy as jnp
        import numpy as np
        N = 4096
        D = 128
        L = 3

        def _cxin_conv(x, a, eps, W, b):
            ax = a @ x
            h = ax + (1.0 + eps[0]) * ax
            for i in range(L):
                h = jax.nn.relu(h @ W[i].T + b[i])
            return h
        out1 = _cxin_conv(x1, G1, eps1, W1, b1)
        out2 = _cxin_conv(x2, G2, eps2, W2, b2)
        merged = jnp.concatenate((out1, out2), axis=1)
        return merged @ Wm.T + bm
    x = _layernorm(x + _L0_gnn_ref(x, L0_gnn_spatial_x, adj, L0_gnn_W_f, L0_gnn_b_f, L0_gnn_W_s, L0_gnn_b_s, L0_gnn_W_att, L0_gnn_b_att), axis=-1)
    x = _layernorm(x + _L1_gnn_ref(x, L1_gnn_x2, adj, adj, L1_gnn_eps1, L1_gnn_eps2, L1_gnn_W1, L1_gnn_b1, L1_gnn_W2, L1_gnn_b2, L1_gnn_Wm, L1_gnn_bm), axis=-1)
    return x

_drawn_inputs = setup_inputs


def setup_inputs(seed=0):
    import zlib

    import numpy as np

    out = dict(_drawn_inputs(seed))
    spreads = {'L1_gnn_b1': (0.0, 0.325), 'L1_gnn_b2': (0.0, 0.331), 'L1_gnn_bm': (0.0, 0.1)}
    factors = {'L0_gnn_W_att': 36.929}
    for name, (base, spread) in spreads.items():
        noise = np.random.default_rng([zlib.crc32(name.encode()), seed]).standard_normal(out[name].shape)
        drawn = base * np.exp(spread * noise) if base else spread * noise
        out[name] = jnp.asarray(drawn.astype(out[name].dtype))
    for name, factor in factors.items():
        out[name] = (out[name] * factor).astype(out[name].dtype)
    return out
```

```python
from contextlib import ExitStack

import numpy as np

import concourse.bass as bass
from concourse import mybir

F32 = mybir.dt.float32
F32R = mybir.dt.float32r
ALU = mybir.AluOpType
ACT = mybir.ActivationFunctionType

P = 128
N = 4096
D = 128
TILES = N // P
CW = 1024
CHUNKS = N // CW
BLOCKS = CW // P
BANK = 512
RAW = 8
SPL = 4
LAYERS = 3
DEG_EPS = 1e-9
LN_EPS = 1e-5

DEG, GCN, CONV = range(3)
SETS = (1, 2, 1)
BANKS = tuple(s * CW // BANK for s in SETS)

WHOLE_DEG = (*range(2, TILES, 2), TILES - 1)
WHOLE_CONV0 = tuple(range(0, 24, 2))

LAYER_SLOTS = {DEG: (3, 10, 17), CONV: (3, 8, 13)}
MERGE_SLOT = {DEG: 24, CONV: 17}

PARAMS = (("w_f", D), ("w_s", D), ("w1", LAYERS * D), ("w2", LAYERS * D), ("wm1", D), ("wm2", D),
          ("b_fs", 2 * D), ("w_att", 2 * D), ("bm", D), ("b1", LAYERS), ("b2", LAYERS),
          ("b_att", 1), ("eps1", 1), ("eps2", 1))
AT, _at = {}, 0
for _name, _width in PARAMS:
    AT[_name] = _at
    _at += _width
PARAM_COLS = _at


def sum_banks(acc, part, c):
    return acc[:, :, :] if part == GCN else acc[:, bass.ds(c % 2 * 2, 2), :]


class Chunk:

    def __init__(self, part, c, peeled):
        self.part, self.c, self.peeled = part, c, peeled
        self.whole = WHOLE_DEG if part == DEG else WHOLE_CONV0 if part == CONV and peeled else ()
        self.split = [j for j in range(TILES) if j not in self.whole]
        self.first = part == DEG and peeled
        self.tiles = c * TILES + part * CHUNKS * TILES
        per_deg = TILES - len(WHOLE_DEG)
        if part == DEG:
            self.splits = c * per_deg
        elif part == GCN:
            self.splits = c * TILES + CHUNKS * per_deg
        elif peeled:
            self.splits = CHUNKS * (per_deg + TILES)
        else:
            self.splits = c * TILES + CHUNKS * (per_deg + TILES) - len(WHOLE_CONV0)
        self.banks = c * BANKS[part] + CHUNKS * sum(BANKS[:part])
        self.early_banks = c * (BANKS[part] - 1) + CHUNKS * sum(b - 1 for b in BANKS[:part])
        self.sums = c * (TILES - 1)

    def loads(self, j):
        c, before = self.c, self.part * CHUNKS * TILES // RAW
        return c * (16 * TILES // RAW) + 16 * (before + j // RAW + 1)

    def splits_done(self, j):
        return self.splits + (self.split.index(j) + 1)

    def sums_done(self, j):
        return self.sums + max(j, 1)

    def tile_done(self, j):
        return self.tiles + (j + 1)


def before(k):
    if k.first:
        return None
    if k.peeled:
        return Chunk(k.part - 1, CHUNKS - 1, False)
    return Chunk(k.part, k.c - 1, False)


def schedule(engine, tiles, tail):
    for part in (DEG, GCN, CONV):
        tiles(Chunk(part, 0, True), None if part == DEG else (part - 1, CHUNKS - 1))
        with engine.Fori(1, CHUNKS) as c:
            tiles(Chunk(part, c, False), (part, c - 1))
    tail(CONV, CHUNKS - 1, None)


def build(nc, adj_t, x_t, s_t, x2_t, params, out_t):
    with ExitStack() as st:
        def sb(name, shape, dt=F32):
            return st.enter_context(nc.sbuf_tensor(name, shape, dt))

        def sem(name):
            return st.enter_context(nc.semaphore(name))

        raw = sb("raw", [P, RAW, CW])
        hi = sb("hi", [P, SPL, CW], F32R)
        lo = sb("lo", [P, SPL, CW], F32R)
        x = sb("x", [P, TILES, D])
        x2 = sb("x2", [P, TILES, D])
        m2 = sb("m2", [P, TILES, D])
        y0_hi = sb("y0_hi", [P, TILES, D], F32R)
        y0_lo = sb("y0_lo", [P, TILES, D], F32R)
        y1_hi = sb("y1_hi", [P, TILES, D], F32R)
        y1_lo = sb("y1_lo", [P, TILES, D], F32R)
        par = sb("par", [P, PARAM_COLS])
        rows = sb("rows", [P, CW])
        ax = sb("ax", [P, CW])
        h = sb("h", [P, 2, CW])
        v = sb("v", [P, BLOCKS, D])
        ones = sb("ones", [P, 1])
        scale = sb("scale", [P, 2])
        deg = sb("deg", [P, BLOCKS])
        deg_root = sb("deg_root", [P, BLOCKS])
        d = sb("d", [P, TILES])
        logit = sb("logit", [P, BLOCKS])
        attn = sb("attn", [P, BLOCKS])
        stats = sb("stats", [P, BLOCKS, 6])
        pair = sb("pair", [P, 5, BLOCKS])
        mean = sb("mean", [P, BLOCKS])
        var = sb("var", [P, BLOCKS])
        std = sb("std", [P, BLOCKS])
        rstd = sb("rstd", [P, BLOCKS])
        shift = sb("shift", [P, BLOCKS])
        msg = x2[:, 0:2 * BLOCKS, :].rearrange("p (k b) f -> p k (b f)", k=4)
        u = x2[:, 2 * BLOCKS:4 * BLOCKS, :].rearrange("p (b k) f -> p b (k f)", k=2)

        def w(name, i=0, n=D):
            return par[:, AT[name] + i * D:AT[name] + i * D + n]

        def col(name, i=0):
            return par[:, AT[name] + i:AT[name] + i + 1]

        acc = st.enter_context(nc.psum_tensor("acc", [P, 4, BANK], F32))
        tp = st.enter_context(nc.psum_tensor("tp", [P, 4, BANK], F32))
        deg_ps = tp[:, 3, 0:BLOCKS]
        pair_ps = tp[:, :, :].rearrange("p k (b f) -> p (k b) f", b=2)

        raw_loaded = [sem(f"raw_loaded{i}") for i in range(RAW)]
        params_loaded = sem("params_loaded")
        x2_loaded = [sem(f"x2_loaded{i}") for i in range(CHUNKS)]
        x_loaded = sem("x_loaded")
        s_loaded = [sem(f"s_loaded{i}") for i in range(CHUNKS)]
        ones_ready = sem("ones_ready")
        scale_ready = sem("scale_ready")
        hi_ready = sem("hi_ready")
        lo_ready = sem("lo_ready")
        y_hi_ready = sem("y_hi_ready")
        y_lo_ready = sem("y_lo_ready")
        rows_summed = sem("rows_summed")
        tile_used = sem("tile_used")
        bank_done = sem("bank_done")
        bank_out = sem("bank_out")
        deg_done = sem("deg_done")
        deg_ready = sem("deg_ready")
        deg_root_ready = sem("deg_root_ready")
        d_ready = sem("d_ready")
        layer_done = sem("layer_done")
        relu_done = sem("relu_done")
        merge_done = sem("merge_done")
        m2_out = sem("m2_out")
        m2_bias = sem("m2_bias")
        base_ready = sem("base_ready")
        pair_done = sem("pair_done")
        u_done = sem("u_done")
        gate_relu_done = sem("gate_relu_done")
        logit_done = sem("logit_done")
        diff_done = sem("diff_done")
        attn_done = sem("attn_done")
        mix_done = sem("mix_done")
        v_done = sem("v_done")
        stats_done = sem("stats_done")
        pair_summed = sem("pair_summed")
        var_parts_done = sem("var_parts_done")
        mean_done = sem("mean_done")
        var_done = sem("var_done")
        std_done = sem("std_done")
        rstd_done = sem("rstd_done")
        x1_ready = sem("x1_ready")
        shift_done = sem("shift_done")
        norm_done = sem("norm_done")
        stored = sem("stored")

        DEG_WHOLE_SPLITS = TILES - len(WHOLE_DEG)

        def y_count(part, j):
            if part == DEG:
                return sum(i not in WHOLE_DEG for i in range(j + 1))
            if part == GCN:
                return DEG_WHOLE_SPLITS + 2 * (j + 1)
            return DEG_WHOLE_SPLITS + 2 * TILES + j + 1

        def lns(part, c):
            return c + (CHUNKS if part == CONV else 0)

        def mlps(part, c):
            return c + (CHUNKS if part == CONV else 0)

        def split_slot_freed(eng, k, j):
            n = k.split.index(j)
            if n >= SPL:
                eng.wait_ge(tile_used, k.tile_done(k.split[n - SPL]))
            elif not k.first:
                b = before(k)
                eng.wait_ge(tile_used, b.tile_done(b.split[n - SPL]))

        block = st.enter_context(nc.Block())

        @block.sync
        def _(sp):
            def tiles(k, prev):
                for j in range(TILES):
                    b, i = (k, j - RAW) if j >= RAW else (before(k), TILES + j - RAW)
                    if b is not None:
                        if i in b.whole:
                            sp.wait_ge(tile_used, b.tile_done(i))
                        elif b.part == DEG:
                            sp.wait_ge(rows_summed, b.sums_done(i))
                        else:
                            sp.wait_ge(lo_ready, b.splits_done(i))
                    sp.dma_start(raw[:, j % RAW, :], adj_t[k.c, j]).then_inc(raw_loaded[j % RAW], 16)

            schedule(sp, tiles, lambda *_: None)

        @block.gpsimd
        def _(pool):
            def split_features(part, j):
                src = x2 if part == DEG else x
                pool.wait_ge(y_hi_ready, y_count(part, j))
                pool.tensor_tensor(y0_lo[:, j, :], src[:, j, :], y0_hi[:, j, :].bitcast(F32), ALU.subtract)\
                    .then_inc(y_lo_ready, 1)

            for j in range(TILES):
                if j not in WHOLE_DEG:
                    split_features(DEG, j)
                if j == BLOCKS:
                    pool.dma_start(par[:, :], params).then_inc(params_loaded, 16)
            pool.wait_ge(tile_used, TILES)
            pool.dma_start(x[:, :, :], x_t).then_inc(x_loaded, 16)
            for n in range(CHUNKS):
                pool.wait_ge(tile_used, (CHUNKS - 1) * TILES + (n + 1) * BLOCKS)
                own = slice(n * BLOCKS, (n + 1) * BLOCKS)
                pool.dma_start(x2[:, own, :], s_t[:, own, :]).then_inc(s_loaded[n], 16)
            for j in range(TILES):
                split_features(CONV, j)

        @block.scalar
        def _(act):
            for n in range(CHUNKS):
                own = slice(n * BLOCKS, (n + 1) * BLOCKS)
                act.dma_start(x2[:, own, :], x2_t[:, own, :]).then_inc(x2_loaded[n], 16)

            def split_tile(k, j):
                act.wait_ge(raw_loaded[j % RAW], k.loads(j))
                split_slot_freed(act, k, j)
                n = k.split.index(j) % SPL
                act.activation(hi[:, n, :], raw[:, j % RAW, :], ACT.Copy).then_inc(hi_ready, 1)

            def split_features(k, j):
                if k.part == DEG:
                    if j in k.whole:
                        return
                    act.wait_ge(x2_loaded[j // BLOCKS], 16)
                    act.activation(y0_hi[:, j, :], x2[:, j, :], ACT.Copy).then_inc(y_hi_ready, 1)
                elif k.part == GCN:
                    act.wait_ge(tile_used, (CHUNKS - 1) * TILES + j + 1)
                    act.wait_ge(d_ready, j // BLOCKS + 1)
                    act.wait_ge(x_loaded, 16)
                    act.activation(y0_hi[:, j, :], x[:, j, :], ACT.Copy, scale=d[:, j:j + 1]).then_inc(y_hi_ready, 1)
                    act.wait_ge(s_loaded[j // BLOCKS], 16)
                    act.activation(y1_hi[:, j, :], x2[:, j, :], ACT.Copy, scale=d[:, j:j + 1]).then_inc(y_hi_ready, 1)
                else:
                    act.wait_ge(tile_used, (2 * CHUNKS - 1) * TILES + j + 1)
                    act.wait_ge(x1_ready, j + 1)
                    act.activation(y0_hi[:, j, :], x[:, j, :], ACT.Copy).then_inc(y_hi_ready, 1)

            def copy_sums(part, c):
                k = Chunk(part, c, False)
                sums = sum_banks(acc, part, c)
                for n in range(BANKS[part]):
                    if n < BANKS[part] - 1:
                        act.wait_ge(bank_done, k.early_banks + (n + 1))
                    else:
                        act.wait_ge(tile_used, k.tile_done(TILES - 1))
                    dst = msg[:, n, :] if part == GCN else ax[:, n * BANK:(n + 1) * BANK]
                    act.activation(dst, sums[:, n, :], ACT.Copy).then_inc(bank_out, 1)

            def relu_layer(part, c, layer):
                b = "b2" if part == DEG else "b1"
                e = 1 if part == DEG else 0
                m = mlps(part, c)
                if layer == 0:
                    act.wait_ge(scale_ready, 1)
                for n in range(2):
                    act.wait_ge(layer_done, m * (2 * LAYERS) + (2 * layer + n + 1))
                    act.activation(h[:, layer % 2, n * BANK:(n + 1) * BANK], tp[:, n, :], ACT.Relu, bias=col(b, layer),
                                   scale=scale[:, e:e + 1] if layer == 0 else 1.0).then_inc(relu_done, 1)

            def root_var(part, c):
                act.wait_ge(var_done, lns(part, c) + 1)
                act.activation(std[:, :], var[:, :], ACT.Sqrt).then_inc(std_done, 1)

            def normalise(c, b):
                act.activation(x2[:, bass.ds(c * BLOCKS + b, 1), :], v[:, b:b + 1, :], ACT.Identity,
                               bias=shift[:, b:b + 1], scale=rstd[:, b:b + 1]).then_inc(norm_done, 1)

            def store(c):
                act.wait_ge(norm_done, c * BLOCKS + BLOCKS)
                act.dma_start(out_t[:, bass.ds(c * BLOCKS, BLOCKS), :],
                              x2[:, bass.ds(c * BLOCKS, BLOCKS), :]).then_inc(stored, 16)

            def tail(part, c, slot):
                def at(n):
                    return slot is None or slot == n

                if at(2 if part == GCN else 3):
                    copy_sums(part, c)
                if part == GCN:
                    if at(9):
                        for q in range(2):
                            act.wait_ge(u_done, c * BLOCKS + 4 * (q + 1))
                            act.activation(u[:, 4 * q:4 * q + 4, :], u[:, 4 * q:4 * q + 4, :], ACT.Relu)\
                               .then_inc(gate_relu_done, 1)
                    if at(12):
                        act.wait_ge(logit_done, c * BLOCKS + BLOCKS)
                        act.activation(attn[:, :], logit[:, :], ACT.Sigmoid, bias=col("b_att")).then_inc(attn_done, 1)
                    if at(19):
                        root_var(part, c)
                    return
                if part == DEG and at(8):
                    act.wait_ge(deg_ready, c + 1)
                    act.activation(deg_root[:, :], deg[:, :], ACT.Sqrt).then_inc(deg_root_ready, 1)
                for layer in range(LAYERS):
                    if at(LAYER_SLOTS[part][layer] + 3):
                        relu_layer(part, c, layer)
                if part == DEG and at(MERGE_SLOT[part] + 3):
                    for q in range(2):
                        act.wait_ge(merge_done, c * 2 + (q + 1))
                        act.activation(m2[:, bass.ds(c * BLOCKS + 4 * q, 4), :], tp[:, 2 + q, :], ACT.Copy)\
                           .then_inc(m2_out, 1)
                if part == CONV:
                    if at(25):
                        root_var(part, c)
                    for n in range(4):
                        if at(27 + n):
                            if n == 0:
                                act.wait_ge(shift_done, c + 1)
                            normalise(c, 2 * n)
                            normalise(c, 2 * n + 1)
                    if at(31):
                        store(c)

            def tiles(k, prev):
                for j in range(TILES):
                    if prev:
                        tail(*prev, j)
                    if k.peeled:
                        split_features(k, j)
                    if j not in k.whole:
                        split_tile(k, j)

            schedule(act, tiles, tail)
            act.wait_ge(stored, 16 * CHUNKS)

        @block.vector
        def _(dve):
            dve.memset(ones[:, :], 1.0).then_inc(ones_ready, 1)

            def split_tile(k, j):
                dve.wait_ge(hi_ready, k.splits_done(j))
                split_slot_freed(dve, k, j)
                n = k.split.index(j) % SPL
                dve.tensor_tensor(lo[:, n, :], raw[:, j % RAW, :], hi[:, n, :].bitcast(F32), ALU.subtract)\
                   .then_inc(lo_ready, 1)

            def split_features(k, j):
                if k.part == GCN:
                    for n, (src, y_hi, y_lo) in enumerate(((x, y0_hi, y0_lo), (x2, y1_hi, y1_lo))):
                        dve.wait_ge(y_hi_ready, y_count(GCN, j) - 1 + n)
                        dve.scalar_tensor_tensor(y_lo[:, j, :], src[:, j, :], d[:, j:j + 1], y_hi[:, j, :].bitcast(F32),
                                                 ALU.mult, ALU.subtract).then_inc(y_lo_ready, 1)

            def sum_rows(k, j):
                if j == 0:
                    return
                if j == 1:
                    dve.wait_ge(raw_loaded[0], k.loads(0))
                dve.wait_ge(raw_loaded[j % RAW], k.loads(j))
                if j > 1:
                    dve.wait_ge(rows_summed, k.sums_done(j - 1))
                elif not k.first:
                    dve.wait_ge(deg_done, k.c)
                first = raw[:, 0, :] if j == 1 else rows[:, :]
                dve.tensor_tensor(rows[:, :], first, raw[:, j % RAW, :], ALU.add).then_inc(rows_summed, 1)

            def v_stats(part, c, q):
                n = lns(part, c)
                dve.wait_ge(v_done, n * 2 + (q + 1))
                for b in range(4 * q, 4 * q + 4):
                    dve.bn_stats(stats[:, b, :], v[:, b, :]).then_inc(stats_done, 1)

            def v_mean_var(part, c):
                n = lns(part, c)
                even, odd = stats[:, :, 0:3], stats[:, :, 3:6]
                dve.wait_ge(stats_done, n * BLOCKS + BLOCKS)
                dve.tensor_tensor(pair[:, 0, :], even[:, :, 1], odd[:, :, 1], ALU.add).then_inc(pair_summed, 1)
                dve.tensor_tensor(pair[:, 1, :], even[:, :, 1], odd[:, :, 1], ALU.subtract).then_inc(pair_summed, 1)
                dve.tensor_tensor(pair[:, 2, :], even[:, :, 2], odd[:, :, 2], ALU.add).then_inc(pair_summed, 1)
                dve.wait_ge(pair_summed, n * 3 + 3)
                dve.tensor_scalar(mean[:, :], pair[:, 0, :], 0.5, None, ALU.mult).then_inc(mean_done, 1)
                dve.scalar_tensor_tensor(pair[:, 3, :], pair[:, 1, :], 0.25, pair[:, 1, :], ALU.mult, ALU.mult)\
                   .then_inc(var_parts_done, 1)
                dve.tensor_scalar(pair[:, 4, :], pair[:, 2, :], 1.0 / D, LN_EPS, ALU.mult, ALU.add)\
                   .then_inc(var_parts_done, 1)
                dve.wait_ge(var_parts_done, n * 2 + 2)
                dve.tensor_tensor(var[:, :], pair[:, 3, :], pair[:, 4, :], ALU.add).then_inc(var_done, 1)

            def inverse_std(part, c):
                dve.wait_ge(std_done, lns(part, c) + 1)
                dve.reciprocal(rstd[:, :], std[:, :]).then_inc(rstd_done, 1)
                dve.wait_ge(rstd_done, lns(part, c) + 1)

            def tail(part, c, slot):
                def at(n):
                    return slot is None or slot == n

                if part == DEG:
                    if at(4):
                        dve.wait_ge(deg_done, c + 1)
                        dve.tensor_scalar(deg[:, :], deg_ps, DEG_EPS, None, ALU.add).then_inc(deg_ready, 1)
                    if at(10):
                        dve.wait_ge(deg_root_ready, c + 1)
                        dve.reciprocal(d[:, bass.ds(c * BLOCKS, BLOCKS)], deg_root[:, :]).then_inc(d_ready, 1)
                if part == GCN:
                    own = bass.ds(c * BLOCKS, BLOCKS)
                    if at(4):
                        dve.wait_ge(m2_out, 2 * CHUNKS)
                        dve.tensor_tensor(m2[:, own, :], m2[:, own, :],
                                          w("bm").rearrange("p (a f) -> p a f", a=1).to_broadcast([P, BLOCKS, D]),
                                          ALU.add).then_inc(m2_bias, 1)
                    for q in range(2):
                        if at(6 + q):
                            for b in range(4 * q, 4 * q + 4):
                                if b % 2 == 0:
                                    dve.wait_ge(pair_done, c * BLOCKS + (b + 2))
                                dve.scalar_tensor_tensor(u[:, b, :], pair_ps[:, b, :], d[:, bass.ds(c * BLOCKS + b, 1)],
                                                         w("b_fs", 0, 2 * D), ALU.mult, ALU.add).then_inc(u_done, 1)
                        if at(9 + q):
                            dve.wait_ge(gate_relu_done, c * 2 + (q + 1))
                            for b in range(4 * q, 4 * q + 4):
                                product = x2[:, 2 * b:2 * b + 2, :].rearrange("p k f -> p (k f)")
                                dve.tensor_tensor_reduce(product, u[:, b, :], w("w_att", 0, 2 * D), 1.0, 0.0,
                                                         ALU.mult, ALU.add, logit[:, b:b + 1]).then_inc(logit_done, 1)
                            half = slice(4 * q, 4 * q + 4)
                            dve.tensor_tensor(v[:, half, :], u[:, half, 0:D], u[:, half, D:2 * D], ALU.subtract)\
                               .then_inc(diff_done, 1)
                        if at(12 + q):
                            dve.wait_ge(attn_done, c + 1)
                            dve.wait_ge(diff_done, c * 2 + (q + 1))
                            for b in range(4 * q, 4 * q + 4):
                                dve.scalar_tensor_tensor(v[:, b, :], v[:, b, :], attn[:, b:b + 1], u[:, b, D:2 * D],
                                                         ALU.mult, ALU.add).then_inc(mix_done, 1)
                        if at(14):
                            dve.wait_ge(mix_done, c * BLOCKS + 4 * (q + 1))
                            half = slice(4 * q, 4 * q + 4)
                            dve.tensor_tensor(v[:, half, :], v[:, half, :], x[:, bass.ds(c * BLOCKS + 4 * q, 4), :],
                                              ALU.add).then_inc(v_done, 1)
                        if at(15 + q):
                            v_stats(part, c, q)
                    if at(17):
                        v_mean_var(part, c)
                    if at(19):
                        inverse_std(part, c)
                    for q in range(2):
                        if at(20 + q):
                            for b in range(4 * q, 4 * q + 4):
                                dve.tensor_scalar(x[:, bass.ds(c * BLOCKS + b, 1), :], v[:, b:b + 1, :], mean[:, b:b + 1],
                                                  rstd[:, b:b + 1], ALU.subtract, ALU.mult).then_inc(x1_ready, 1)
                    if at(22):
                        dve.wait_ge(x1_ready, c * BLOCKS + BLOCKS)
                        dve.wait_ge(m2_bias, c + 1)
                        dve.tensor_tensor(m2[:, own, :], m2[:, own, :], x[:, own, :], ALU.add).then_inc(base_ready, 1)
                if part == CONV:
                    for q in range(2):
                        if at(20):
                            dve.wait_ge(base_ready, CHUNKS)
                            dve.wait_ge(merge_done, c * 2 + (2 * CHUNKS + q + 1))
                            dve.tensor_tensor(v[:, 4 * q:4 * q + 4, :], tp[:, 2 + q, :].rearrange("p (b f) -> p b f", b=4),
                                              m2[:, bass.ds(c * BLOCKS + 4 * q, 4), :], ALU.add).then_inc(v_done, 1)
                    for q in range(2):
                        if at(21 + q):
                            v_stats(part, c, q)
                    if at(23):
                        v_mean_var(part, c)
                    if at(25):
                        inverse_std(part, c)
                        dve.scalar_tensor_tensor(shift[:, :], mean[:, :], -1.0, rstd[:, :], ALU.mult, ALU.mult)\
                           .then_inc(shift_done, 1)

            def tiles(k, prev):
                for j in range(TILES):
                    if prev:
                        tail(*prev, j)
                    if k.peeled:
                        split_features(k, j)
                    if j not in k.whole:
                        split_tile(k, j)
                    if k.part == DEG:
                        sum_rows(k, j)
                    if k.first and j == TILES - 4:
                        dve.wait_ge(params_loaded, 16)
                        dve.tensor_scalar(scale[:, :], par[:, AT["eps1"]:AT["eps1"] + 2], 2.0, None, ALU.add)\
                           .then_inc(scale_ready, 1)

            schedule(dve, tiles, tail)

        @block.tensor
        def _(pe):
            def multiply(k, j):
                if j in k.whole:
                    pe.wait_ge(raw_loaded[j % RAW], k.loads(j))
                    if k.part == DEG:
                        pe.wait_ge(x2_loaded[j // BLOCKS], 16)
                        pe.wait_ge(rows_summed, k.sums_done(j))
                        plain = x2
                    else:
                        pe.wait_ge(x1_ready, j + 1)
                        plain = x
                else:
                    pe.wait_ge(lo_ready, k.splits_done(j))
                    if k.peeled:
                        pe.wait_ge(y_lo_ready, y_count(k.part, j))
                n = k.split.index(j) % SPL if j in k.split else None
                prior = before(k)
                sums = sum_banks(acc, k.part, k.c)
                for bank in range(BANKS[k.part]):
                    out = sums[:, bank, :]
                    cols = slice(bank % 2 * BANK, (bank % 2 + 1) * BANK)
                    first, last = j == 0, j == TILES - 1
                    if first and k.part != DEG and (k.peeled or k.part == GCN):
                        pe.wait_ge(bank_out, prior.banks + (bank % BANKS[prior.part] + 1))
                    if n is None:
                        mm = pe.matmul(out, plain[:, j, :], raw[:, j % RAW, cols], start=first, stop=last)
                    else:
                        y_hi, y_lo = ((y0_hi, y0_lo), (y1_hi, y1_lo))[bank // 2]
                        pe.matmul(out, y_hi[:, j, :], hi[:, n, cols], start=first, stop=False)
                        pe.matmul(out, y_lo[:, j, :], hi[:, n, cols], start=False, stop=False)
                        mm = pe.matmul(out, y_hi[:, j, :], lo[:, n, cols], start=False, stop=last)
                    if bank == BANKS[k.part] - 1:
                        mm.then_inc(tile_used, 1)
                    elif last:
                        mm.then_inc(bank_done, 1)

            def layer(part, c, n_layer):
                weights = w("w2" if part == DEG else "w1", n_layer)
                k = Chunk(part, c, False)
                if part == CONV and n_layer == 0:
                    pe.wait_ge(u_done, CHUNKS * BLOCKS)
                pe.wait_ge(params_loaded, 16)
                for n in range(2):
                    if n_layer == 0:
                        pe.wait_ge(bank_out, k.banks + (n + 1))
                        src = ax
                    else:
                        pe.wait_ge(relu_done, mlps(part, c) * (2 * LAYERS) + (2 * n_layer - 2 + n + 1))
                        src = h[:, (n_layer - 1) % 2, :]
                    pe.matmul(tp[:, n, :], weights, src[:, n * BANK:(n + 1) * BANK], start=True, stop=True)\
                      .then_inc(layer_done, 1)

            def merge(part, c):
                weights = w("wm2" if part == DEG else "wm1")
                if part == DEG:
                    pe.wait_ge(deg_ready, c + 1)
                for b in range(BLOCKS):
                    if b % 4 == 0:
                        pe.wait_ge(relu_done, mlps(part, c) * (2 * LAYERS) + (2 * LAYERS - 2 + b // 4 + 1))
                    mm = pe.matmul(tp[:, 2 + b // 4, b % 4 * D:(b % 4 + 1) * D], h[:, 0, b * P:(b + 1) * P], weights,
                                   start=True, stop=True)
                    if b % 4 == 3:
                        mm.then_inc(merge_done, 1)

            def tail(part, c, slot):
                def at(n):
                    return slot is None or slot == n

                if part == DEG and at(0):
                    pe.wait_ge(ones_ready, 1)
                    pe.wait_ge(rows_summed, c * (TILES - 1) + (TILES - 1))
                    for b in range(BLOCKS):
                        mm = pe.matmul(deg_ps[:, b:b + 1], rows[:, b * P:(b + 1) * P], ones[:, :], start=True, stop=True)
                    mm.then_inc(deg_done, 1)
                if part == GCN:
                    if at(3):
                        pe.wait_ge(bank_out, c * BANKS[GCN] + (CHUNKS * BANKS[DEG] + BANKS[GCN]))
                        pe.wait_ge(m2_out, 2 * CHUNKS)
                        for b in range(BLOCKS):
                            rows_of = slice(b % 4 * P, (b % 4 + 1) * P)
                            pe.matmul(pair_ps[:, b, 0:D], msg[:, b // 4, rows_of], w("w_f"), start=True, stop=True)
                            pe.matmul(pair_ps[:, b, D:2 * D], msg[:, 2 + b // 4, rows_of], w("w_s"),
                                      start=True, stop=True).then_inc(pair_done, 1)
                    return
                for n in range(LAYERS):
                    if at(LAYER_SLOTS[part][n]):
                        layer(part, c, n)
                if at(MERGE_SLOT[part]):
                    merge(part, c)

            def tiles(k, prev):
                for j in range(TILES):
                    if prev:
                        tail(*prev, j)
                    multiply(k, j)

            schedule(pe, tiles, tail)


def kernel(**inputs):
    import concourse.bacc as bacc
    from concourse.bass_utils import run_bass_kernel_spmd

    def rep(a):
        return np.broadcast_to(np.asarray(a).reshape(1, -1), (P, np.asarray(a).size))

    def by_block(a):
        return np.ascontiguousarray(np.asarray(a).reshape(TILES, P, D).transpose(1, 0, 2))

    def layers(a):
        return np.asarray(a).transpose(2, 0, 1).reshape(D, LAYERS * D)

    adj = np.asarray(inputs["adj"])
    wm = np.asarray(inputs["L1_gnn_Wm"])
    arrays = {
        "adj_t": np.ascontiguousarray(adj.reshape(CHUNKS, CW, TILES, P).transpose(0, 2, 3, 1)),
        "x_t": by_block(inputs["x"]),
        "s_t": by_block(inputs["L0_gnn_spatial_x"]),
        "x2_t": by_block(inputs["L1_gnn_x2"]),
        "params": np.ascontiguousarray(np.concatenate([
            np.asarray(inputs["L0_gnn_W_f"]), np.asarray(inputs["L0_gnn_W_s"]),
            layers(inputs["L1_gnn_W1"]), layers(inputs["L1_gnn_W2"]), wm[:, :D].T, wm[:, D:].T,
            rep(inputs["L0_gnn_b_f"]), rep(inputs["L0_gnn_b_s"]), rep(inputs["L0_gnn_W_att"]), rep(inputs["L1_gnn_bm"]),
            np.asarray(inputs["L1_gnn_b1"]).T, np.asarray(inputs["L1_gnn_b2"]).T,
            rep(inputs["L0_gnn_b_att"]), rep(inputs["L1_gnn_eps1"]), rep(inputs["L1_gnn_eps2"])], axis=1)),
    }
    nc = bacc.Bacc("TRN2", target_bir_lowering=False, num_devices=1)
    aps = [nc.dram_tensor(n, a.shape, mybir.dt.from_np(a.dtype), kind="ExternalInput").ap() for n, a in arrays.items()]
    out = nc.dram_tensor("out_t", (P, TILES, D), F32, kind="ExternalOutput").ap()
    build(nc, *aps, out)
    r = run_bass_kernel_spmd(nc, [arrays], core_ids=[0])
    got = r.results[0]["out_t"]
    return np.ascontiguousarray(np.asarray(got).transpose(1, 0, 2).reshape(N, D))
```

```python
from contextlib import ExitStack

import numpy as np

import concourse.bass as bass
from concourse import mybir

F32 = mybir.dt.float32
F32R = mybir.dt.float32r
ALU = mybir.AluOpType
ACT = mybir.ActivationFunctionType

P = 128
N = 4096
D = 128
TILES = N // P
CW = 1024
CHUNKS = N // CW
BLOCKS = CW // P
BANK = 512
RAW = 8
SPL = 4
LAYERS = 3
DEG_EPS = 1e-9
LN_EPS = 1e-5

DEG, GCN, CONV = range(3)
SETS = (1, 2, 1)
BANKS = tuple(s * CW // BANK for s in SETS)

WHOLE_DEG = tuple(j for j in range(2, TILES) if j % 3 != 1)
WHOLE_CONV0 = tuple(range(0, 24, 2))

LAYER_SLOTS = {GCN: (11, 17, 23), CONV: (3, 8, 13)}
MERGE_SLOT = {GCN: 28, CONV: 17}

PARAMS = (("w_f", D), ("w_s", D), ("w1", LAYERS * D), ("wm1", D), ("wm2", D),
          ("b_fs", 2 * D), ("w_att", 2 * D), ("bm", D), ("b1", LAYERS), ("b2", LAYERS),
          ("b_att", 1), ("eps1", 1), ("eps2", 1))
AT, _at = {}, 0
for _name, _width in PARAMS:
    AT[_name] = _at
    _at += _width
PARAM_COLS = _at


def sum_banks(acc, part, c):
    return acc[:, :, :] if part == GCN else acc[:, bass.ds(c % 2 * 2, 2), :]


class Chunk:

    def __init__(self, part, c, peeled):
        self.part, self.c, self.peeled = part, c, peeled
        self.whole = WHOLE_DEG if part == DEG else WHOLE_CONV0 if part == CONV and peeled else ()
        self.split = [j for j in range(TILES) if j not in self.whole]
        self.first = part == DEG and peeled
        self.tiles = c * TILES + part * CHUNKS * TILES
        per_deg = TILES - len(WHOLE_DEG)
        if part == DEG:
            self.splits = c * per_deg
        elif part == GCN:
            self.splits = c * TILES + CHUNKS * per_deg
        elif peeled:
            self.splits = CHUNKS * (per_deg + TILES)
        else:
            self.splits = c * TILES + CHUNKS * (per_deg + TILES) - len(WHOLE_CONV0)
        self.banks = c * BANKS[part] + CHUNKS * sum(BANKS[:part])
        self.early_banks = c * (BANKS[part] - 1) + CHUNKS * sum(b - 1 for b in BANKS[:part])
        self.sums = c * (TILES - 1)

    def loads(self, j):
        c, before = self.c, self.part * CHUNKS * TILES // RAW
        return c * (16 * TILES // RAW) + 16 * (before + j // RAW + 1)

    def splits_done(self, j):
        return self.splits + (self.split.index(j) + 1)

    def sums_done(self, j):
        return self.sums + max(j, 1)

    def tile_done(self, j):
        return self.tiles + (j + 1)


def before(k):
    if k.first:
        return None
    if k.peeled:
        return Chunk(k.part - 1, CHUNKS - 1, False)
    return Chunk(k.part, k.c - 1, False)


def schedule(engine, tiles, tail):
    for part in (DEG, GCN, CONV):
        tiles(Chunk(part, 0, True), None if part == DEG else (part - 1, CHUNKS - 1))
        with engine.Fori(1, CHUNKS) as c:
            tiles(Chunk(part, c, False), (part, c - 1))
    tail(CONV, CHUNKS - 1, None)


def build(nc, adj_t, x_t, s_t, x2_t, w2_t, params, out_t):
    with ExitStack() as st:
        def sb(name, shape, dt=F32):
            return st.enter_context(nc.sbuf_tensor(name, shape, dt))

        def sem(name):
            return st.enter_context(nc.semaphore(name))

        raw = sb("raw", [P, RAW, CW])
        hi = sb("hi", [P, SPL, CW], F32R)
        lo = sb("lo", [P, SPL, CW], F32R)
        x = sb("x", [P, TILES, D])
        x2 = sb("x2", [P, TILES, D])
        m2 = sb("m2", [P, TILES, D])
        y0_hi = sb("y0_hi", [P, TILES, D], F32R)
        y0_lo = sb("y0_lo", [P, TILES, D], F32R)
        y1_hi = sb("y1_hi", [P, TILES, D], F32R)
        y1_lo = sb("y1_lo", [P, TILES, D], F32R)
        par = sb("par", [P, PARAM_COLS])
        rows = sb("rows", [P, CW])
        h = sb("h", [P, CW])
        h_hi = sb("h_hi", [P, CW], F32R)
        h_lo = sb("h_lo", [P, CW], F32R)
        w2_hi = sb("w2_hi", [P, LAYERS * D], F32R)
        w2_lo = sb("w2_lo", [P, LAYERS * D], F32R)
        v = sb("v", [P, BLOCKS, D])
        ones = sb("ones", [P, 1])
        scale = sb("scale", [P, 2])
        deg = sb("deg", [P, BLOCKS])
        deg_root = sb("deg_root", [P, BLOCKS])
        d = sb("d", [P, TILES])
        logit = sb("logit", [P, BLOCKS])
        attn = sb("attn", [P, BLOCKS])
        stats = sb("stats", [P, BLOCKS, 6])
        pair = sb("pair", [P, 5, BLOCKS])
        mean = sb("mean", [P, BLOCKS])
        var = sb("var", [P, BLOCKS])
        std = sb("std", [P, BLOCKS])
        rstd = sb("rstd", [P, BLOCKS])
        shift = sb("shift", [P, BLOCKS])
        msg = x2[:, 0:2 * BLOCKS, :].rearrange("p (k b) f -> p k (b f)", k=4)
        u = x2[:, 2 * BLOCKS:4 * BLOCKS, :].rearrange("p (b k) f -> p b (k f)", k=2)

        def w(name, i=0, n=D):
            return par[:, AT[name] + i * D:AT[name] + i * D + n]

        def col(name, i=0):
            return par[:, AT[name] + i:AT[name] + i + 1]

        acc = st.enter_context(nc.psum_tensor("acc", [P, 4, BANK], F32))
        tp = st.enter_context(nc.psum_tensor("tp", [P, 4, BANK], F32))
        deg_ps = tp[:, 3, 0:BLOCKS]
        pair_ps = tp[:, :, :].rearrange("p k (b f) -> p (k b) f", b=2)

        raw_loaded = [sem(f"raw_loaded{i}") for i in range(RAW)]
        params_loaded = sem("params_loaded")
        x2_loaded = [sem(f"x2_loaded{i}") for i in range(CHUNKS)]
        x_loaded = sem("x_loaded")
        s_loaded = [sem(f"s_loaded{i}") for i in range(CHUNKS)]
        ones_ready = sem("ones_ready")
        scale_ready = sem("scale_ready")
        hi_ready = sem("hi_ready")
        lo_ready = sem("lo_ready")
        y_hi_ready = sem("y_hi_ready")
        y_lo_ready = sem("y_lo_ready")
        rows_summed = sem("rows_summed")
        tile_used = sem("tile_used")
        bank_done = sem("bank_done")
        bank_out = sem("bank_out")
        deg_done = sem("deg_done")
        deg_ready = sem("deg_ready")
        deg_root_ready = sem("deg_root_ready")
        d_ready = sem("d_ready")
        w2_loaded = sem("w2_loaded")
        w2_hi_ready = sem("w2_hi_ready")
        w2_lo_ready = sem("w2_lo_ready")
        h_hi_ready = sem("h_hi_ready")
        h_lo_ready = sem("h_lo_ready")
        layer_done = sem("layer_done")
        relu_done = sem("relu_done")
        merge_done = sem("merge_done")
        merged = sem("merged")
        base_ready = sem("base_ready")
        pair_done = sem("pair_done")
        u_done = sem("u_done")
        gate_relu_done = sem("gate_relu_done")
        logit_done = sem("logit_done")
        diff_done = sem("diff_done")
        attn_done = sem("attn_done")
        mix_done = sem("mix_done")
        v_done = sem("v_done")
        stats_done = sem("stats_done")
        pair_summed = sem("pair_summed")
        var_parts_done = sem("var_parts_done")
        mean_done = sem("mean_done")
        var_done = sem("var_done")
        std_done = sem("std_done")
        rstd_done = sem("rstd_done")
        x1_ready = sem("x1_ready")
        shift_done = sem("shift_done")
        norm_done = sem("norm_done")
        stored = sem("stored")

        DEG_WHOLE_SPLITS = TILES - len(WHOLE_DEG)

        def y_count(part, j):
            if part == DEG:
                return sum(i not in WHOLE_DEG for i in range(j + 1))
            if part == GCN:
                return DEG_WHOLE_SPLITS + 2 * (j + 1)
            return DEG_WHOLE_SPLITS + 2 * TILES + j + 1

        def lns(part, c):
            return c + (CHUNKS if part == CONV else 0)

        def halves(part, c):
            return (c + (CHUNKS if part == CONV else 0)) * (2 * LAYERS)

        def split_slot_freed(eng, k, j):
            n = k.split.index(j)
            if n >= SPL:
                eng.wait_ge(tile_used, k.tile_done(k.split[n - SPL]))
            elif not k.first:
                b = before(k)
                eng.wait_ge(tile_used, b.tile_done(b.split[n - SPL]))

        block = st.enter_context(nc.Block())

        @block.sync
        def _(sp):
            def tiles(k, prev):
                for j in range(TILES):
                    b, i = (k, j - RAW) if j >= RAW else (before(k), TILES + j - RAW)
                    if b is not None:
                        if i in b.whole:
                            sp.wait_ge(tile_used, b.tile_done(i))
                        elif b.part == DEG:
                            sp.wait_ge(rows_summed, b.sums_done(i))
                        else:
                            sp.wait_ge(lo_ready, b.splits_done(i))
                    sp.dma_start(raw[:, j % RAW, :], adj_t[k.c, j]).then_inc(raw_loaded[j % RAW], 16)

            schedule(sp, tiles, lambda *_: None)

        @block.gpsimd
        def _(pool):
            def split_features(part, j):
                src = x2 if part == DEG else x
                pool.wait_ge(y_hi_ready, y_count(part, j))
                pool.tensor_tensor(y0_lo[:, j, :], src[:, j, :], y0_hi[:, j, :].bitcast(F32), ALU.subtract)\
                    .then_inc(y_lo_ready, 1)

            for j in range(TILES):
                if j not in WHOLE_DEG:
                    split_features(DEG, j)
            pool.wait_ge(tile_used, TILES)
            pool.dma_start(h[:, 0:LAYERS * D], w2_t).then_inc(w2_loaded, 16)
            pool.dma_start(par[:, :], params).then_inc(params_loaded, 16)
            pool.wait_ge(tile_used, TILES + BLOCKS)
            pool.dma_start(x[:, :, :], x_t).then_inc(x_loaded, 16)
            for n in range(CHUNKS):
                pool.wait_ge(tile_used, (CHUNKS - 1) * TILES + (n + 1) * BLOCKS)
                own = slice(n * BLOCKS, (n + 1) * BLOCKS)
                pool.dma_start(x2[:, own, :], s_t[:, own, :]).then_inc(s_loaded[n], 16)
            for j in range(TILES):
                split_features(CONV, j)

        @block.scalar
        def _(act):
            for n in range(CHUNKS):
                own = slice(n * BLOCKS, (n + 1) * BLOCKS)
                act.dma_start(x2[:, own, :], x2_t[:, own, :]).then_inc(x2_loaded[n], 16)

            def split_tile(k, j):
                act.wait_ge(raw_loaded[j % RAW], k.loads(j))
                split_slot_freed(act, k, j)
                n = k.split.index(j) % SPL
                act.activation(hi[:, n, :], raw[:, j % RAW, :], ACT.Copy).then_inc(hi_ready, 1)

            def split_features(k, j):
                if k.part == DEG:
                    if j in k.whole:
                        return
                    act.wait_ge(x2_loaded[j // BLOCKS], 16)
                    act.activation(y0_hi[:, j, :], x2[:, j, :], ACT.Copy).then_inc(y_hi_ready, 1)
                elif k.part == GCN:
                    act.wait_ge(tile_used, (CHUNKS - 1) * TILES + j + 1)
                    act.wait_ge(d_ready, j // BLOCKS + 1)
                    act.wait_ge(x_loaded, 16)
                    act.activation(y0_hi[:, j, :], x[:, j, :], ACT.Copy, scale=d[:, j:j + 1]).then_inc(y_hi_ready, 1)
                    act.wait_ge(s_loaded[j // BLOCKS], 16)
                    act.activation(y1_hi[:, j, :], x2[:, j, :], ACT.Copy, scale=d[:, j:j + 1]).then_inc(y_hi_ready, 1)
                else:
                    act.wait_ge(tile_used, (2 * CHUNKS - 1) * TILES + j + 1)
                    act.wait_ge(x1_ready, j + 1)
                    act.activation(y0_hi[:, j, :], x[:, j, :], ACT.Copy).then_inc(y_hi_ready, 1)

            def copy_sums(part, c):
                k = Chunk(part, c, False)
                sums = sum_banks(acc, part, c)
                for n in range(BANKS[part]):
                    if n < BANKS[part] - 1:
                        act.wait_ge(bank_done, k.early_banks + (n + 1))
                    else:
                        act.wait_ge(tile_used, k.tile_done(TILES - 1))
                    if part == DEG:
                        dst = m2[:, bass.ds(c * BLOCKS + 4 * n, 4), :].rearrange("p b f -> p (b f)")
                    else:
                        dst = msg[:, n, :] if part == GCN else rows[:, n * BANK:(n + 1) * BANK]
                    act.activation(dst, sums[:, n, :], ACT.Copy).then_inc(bank_out, 1)

            def split_w2():
                act.wait_ge(w2_loaded, 16)
                act.activation(w2_hi[:, :], h[:, 0:LAYERS * D], ACT.Copy).then_inc(w2_hi_ready, 1)

            def split_ax2(c):
                for n in range(2):
                    act.activation(h_hi[:, n * BANK:(n + 1) * BANK], m2[:, bass.ds(c * BLOCKS + 4 * n, 4), :], ACT.Copy)\
                       .then_inc(h_hi_ready, 1)

            def relu_layer2(c, layer):
                by = scale[:, 1:2] if layer == 0 else 1.0
                if layer == 0:
                    act.wait_ge(scale_ready, 1)
                    act.wait_ge(w2_lo_ready, 1)
                for n in range(2):
                    half = slice(n * BANK, (n + 1) * BANK)
                    act.wait_ge(layer_done, halves(GCN, c) + (2 * layer + n + 1))
                    act.activation(h[:, half], tp[:, n, :], ACT.Relu, bias=col("b2", layer), scale=by).then_inc(relu_done, 1)
                    if layer < LAYERS - 1:
                        act.activation(h_hi[:, half], tp[:, n, :], ACT.Relu, bias=col("b2", layer), scale=by)\
                           .then_inc(h_hi_ready, 1)

            def branch2(c, slot):
                if slot == 5:
                    if isinstance(c, int):
                        split_w2()
                    split_ax2(c)
                for layer in range(LAYERS):
                    if slot == LAYER_SLOTS[GCN][layer] + 3:
                        relu_layer2(c, layer)

            def relu_layer1(c, layer):
                dst = (h, rows)[layer % 2]
                for n in range(2):
                    act.wait_ge(layer_done, halves(CONV, c) + (2 * layer + n + 1))
                    act.activation(dst[:, n * BANK:(n + 1) * BANK], tp[:, n, :], ACT.Relu, bias=col("b1", layer),
                                   scale=scale[:, 0:1] if layer == 0 else 1.0).then_inc(relu_done, 1)

            def root_var(part, c):
                act.wait_ge(var_done, lns(part, c) + 1)
                act.activation(std[:, :], var[:, :], ACT.Sqrt).then_inc(std_done, 1)

            def normalise(c, b):
                act.activation(x2[:, bass.ds(c * BLOCKS + b, 1), :], v[:, b:b + 1, :], ACT.Identity,
                               bias=shift[:, b:b + 1], scale=rstd[:, b:b + 1]).then_inc(norm_done, 1)

            def store(c):
                act.wait_ge(norm_done, c * BLOCKS + BLOCKS)
                act.dma_start(out_t[:, bass.ds(c * BLOCKS, BLOCKS), :],
                              x2[:, bass.ds(c * BLOCKS, BLOCKS), :]).then_inc(stored, 16)

            def tail(part, c, slot):
                def at(n):
                    return slot is None or slot == n

                if at(2 if part == GCN else 3):
                    copy_sums(part, c)
                if part == GCN:
                    if at(9):
                        for q in range(2):
                            act.wait_ge(u_done, c * BLOCKS + 4 * (q + 1))
                            act.activation(u[:, 4 * q:4 * q + 4, :], u[:, 4 * q:4 * q + 4, :], ACT.Relu)\
                               .then_inc(gate_relu_done, 1)
                    if at(12):
                        act.wait_ge(logit_done, c * BLOCKS + BLOCKS)
                        act.activation(attn[:, :], logit[:, :], ACT.Sigmoid, bias=col("b_att")).then_inc(attn_done, 1)
                    if at(19):
                        root_var(part, c)
                    return
                if part == DEG and at(8):
                    act.wait_ge(deg_ready, c + 1)
                    act.activation(deg_root[:, :], deg[:, :], ACT.Sqrt).then_inc(deg_root_ready, 1)
                if part == CONV:
                    for layer in range(LAYERS):
                        if at(LAYER_SLOTS[CONV][layer] + 3):
                            relu_layer1(c, layer)
                    if at(25):
                        root_var(part, c)
                    for n in range(4):
                        if at(27 + n):
                            if n == 0:
                                act.wait_ge(shift_done, c + 1)
                            normalise(c, 2 * n)
                            normalise(c, 2 * n + 1)
                    if at(31):
                        store(c)

            def tiles(k, prev):
                for j in range(TILES):
                    if prev:
                        tail(*prev, j)
                    if k.part == GCN:
                        branch2(k.c, j)
                    if k.peeled:
                        split_features(k, j)
                    if j not in k.whole:
                        split_tile(k, j)

            schedule(act, tiles, tail)
            act.wait_ge(stored, 16 * CHUNKS)

        @block.vector
        def _(dve):
            dve.memset(ones[:, :], 1.0).then_inc(ones_ready, 1)

            def split_tile(k, j):
                dve.wait_ge(hi_ready, k.splits_done(j))
                split_slot_freed(dve, k, j)
                n = k.split.index(j) % SPL
                dve.tensor_tensor(lo[:, n, :], raw[:, j % RAW, :], hi[:, n, :].bitcast(F32), ALU.subtract)\
                   .then_inc(lo_ready, 1)

            def split_features(k, j):
                if k.part == GCN:
                    for n, (src, y_hi, y_lo) in enumerate(((x, y0_hi, y0_lo), (x2, y1_hi, y1_lo))):
                        dve.wait_ge(y_hi_ready, y_count(GCN, j) - 1 + n)
                        dve.scalar_tensor_tensor(y_lo[:, j, :], src[:, j, :], d[:, j:j + 1], y_hi[:, j, :].bitcast(F32),
                                                 ALU.mult, ALU.subtract).then_inc(y_lo_ready, 1)

            def sum_rows(k, j):
                if j == 0:
                    return
                if j == 1:
                    dve.wait_ge(raw_loaded[0], k.loads(0))
                dve.wait_ge(raw_loaded[j % RAW], k.loads(j))
                if j > 1:
                    dve.wait_ge(rows_summed, k.sums_done(j - 1))
                elif not k.first:
                    dve.wait_ge(deg_done, k.c)
                first = raw[:, 0, :] if j == 1 else rows[:, :]
                dve.tensor_tensor(rows[:, :], first, raw[:, j % RAW, :], ALU.add).then_inc(rows_summed, 1)

            def split_w2():
                dve.wait_ge(w2_hi_ready, 1)
                dve.tensor_tensor(w2_lo[:, :], h[:, 0:LAYERS * D], w2_hi[:, :].bitcast(F32), ALU.subtract)\
                   .then_inc(w2_lo_ready, 1)

            def branch2(c, slot):
                if slot == 5 and isinstance(c, int):
                    split_w2()
                for layer in range(LAYERS):
                    if slot == (5, LAYER_SLOTS[GCN][0] + 4, LAYER_SLOTS[GCN][1] + 4)[layer]:
                        for n in range(2):
                            half = slice(n * BANK, (n + 1) * BANK)
                            src = h[:, half] if layer else m2[:, bass.ds(c * BLOCKS + 4 * n, 4), :]
                            dve.wait_ge(h_hi_ready, halves(GCN, c) + (2 * layer + n + 1))
                            dve.tensor_tensor(h_lo[:, half], src, h_hi[:, half].bitcast(F32), ALU.subtract)\
                               .then_inc(h_lo_ready, 1)
                if slot == TILES - 1:
                    bm = w("bm").rearrange("p (a f) -> p a f", a=1).to_broadcast([P, 4, D])
                    for q in range(2):
                        dve.wait_ge(merge_done, c * 2 + (q + 1))
                        dve.tensor_tensor(m2[:, bass.ds(c * BLOCKS + 4 * q, 4), :],
                                          tp[:, 2 + q, :].rearrange("p (b f) -> p b f", b=4), bm, ALU.add)\
                           .then_inc(merged, 1)

            def v_stats(part, c, q):
                n = lns(part, c)
                dve.wait_ge(v_done, n * 2 + (q + 1))
                for b in range(4 * q, 4 * q + 4):
                    dve.bn_stats(stats[:, b, :], v[:, b, :]).then_inc(stats_done, 1)

            def v_mean_var(part, c):
                n = lns(part, c)
                even, odd = stats[:, :, 0:3], stats[:, :, 3:6]
                dve.wait_ge(stats_done, n * BLOCKS + BLOCKS)
                dve.tensor_tensor(pair[:, 0, :], even[:, :, 1], odd[:, :, 1], ALU.add).then_inc(pair_summed, 1)
                dve.tensor_tensor(pair[:, 1, :], even[:, :, 1], odd[:, :, 1], ALU.subtract).then_inc(pair_summed, 1)
                dve.tensor_tensor(pair[:, 2, :], even[:, :, 2], odd[:, :, 2], ALU.add).then_inc(pair_summed, 1)
                dve.wait_ge(pair_summed, n * 3 + 3)
                dve.tensor_scalar(mean[:, :], pair[:, 0, :], 0.5, None, ALU.mult).then_inc(mean_done, 1)
                dve.scalar_tensor_tensor(pair[:, 3, :], pair[:, 1, :], 0.25, pair[:, 1, :], ALU.mult, ALU.mult)\
                   .then_inc(var_parts_done, 1)
                dve.tensor_scalar(pair[:, 4, :], pair[:, 2, :], 1.0 / D, LN_EPS, ALU.mult, ALU.add)\
                   .then_inc(var_parts_done, 1)
                dve.wait_ge(var_parts_done, n * 2 + 2)
                dve.tensor_tensor(var[:, :], pair[:, 3, :], pair[:, 4, :], ALU.add).then_inc(var_done, 1)

            def inverse_std(part, c):
                dve.wait_ge(std_done, lns(part, c) + 1)
                dve.reciprocal(rstd[:, :], std[:, :]).then_inc(rstd_done, 1)
                dve.wait_ge(rstd_done, lns(part, c) + 1)

            def tail(part, c, slot):
                def at(n):
                    return slot is None or slot == n

                if part == DEG:
                    if at(4):
                        dve.wait_ge(deg_done, c + 1)
                        dve.tensor_scalar(deg[:, :], deg_ps, DEG_EPS, None, ALU.add).then_inc(deg_ready, 1)
                    if at(10):
                        dve.wait_ge(deg_root_ready, c + 1)
                        dve.reciprocal(d[:, bass.ds(c * BLOCKS, BLOCKS)], deg_root[:, :]).then_inc(d_ready, 1)
                if part == GCN:
                    own = bass.ds(c * BLOCKS, BLOCKS)
                    for q in range(2):
                        if at(6 + q):
                            for b in range(4 * q, 4 * q + 4):
                                if b % 2 == 0:
                                    dve.wait_ge(pair_done, c * BLOCKS + (b + 2))
                                dve.scalar_tensor_tensor(u[:, b, :], pair_ps[:, b, :], d[:, bass.ds(c * BLOCKS + b, 1)],
                                                         w("b_fs", 0, 2 * D), ALU.mult, ALU.add).then_inc(u_done, 1)
                        if at(9 + q):
                            dve.wait_ge(gate_relu_done, c * 2 + (q + 1))
                            for b in range(4 * q, 4 * q + 4):
                                product = x2[:, 2 * b:2 * b + 2, :].rearrange("p k f -> p (k f)")
                                dve.tensor_tensor_reduce(product, u[:, b, :], w("w_att", 0, 2 * D), 1.0, 0.0,
                                                         ALU.mult, ALU.add, logit[:, b:b + 1]).then_inc(logit_done, 1)
                            half = slice(4 * q, 4 * q + 4)
                            dve.tensor_tensor(v[:, half, :], u[:, half, 0:D], u[:, half, D:2 * D], ALU.subtract)\
                               .then_inc(diff_done, 1)
                        if at(12 + q):
                            dve.wait_ge(attn_done, c + 1)
                            dve.wait_ge(diff_done, c * 2 + (q + 1))
                            for b in range(4 * q, 4 * q + 4):
                                dve.scalar_tensor_tensor(v[:, b, :], v[:, b, :], attn[:, b:b + 1], u[:, b, D:2 * D],
                                                         ALU.mult, ALU.add).then_inc(mix_done, 1)
                        if at(14):
                            dve.wait_ge(mix_done, c * BLOCKS + 4 * (q + 1))
                            half = slice(4 * q, 4 * q + 4)
                            dve.tensor_tensor(v[:, half, :], v[:, half, :], x[:, bass.ds(c * BLOCKS + 4 * q, 4), :],
                                              ALU.add).then_inc(v_done, 1)
                        if at(15 + q):
                            v_stats(part, c, q)
                    if at(17):
                        v_mean_var(part, c)
                    if at(19):
                        inverse_std(part, c)
                    for q in range(2):
                        if at(20 + q):
                            for b in range(4 * q, 4 * q + 4):
                                dve.tensor_scalar(x[:, bass.ds(c * BLOCKS + b, 1), :], v[:, b:b + 1, :], mean[:, b:b + 1],
                                                  rstd[:, b:b + 1], ALU.subtract, ALU.mult).then_inc(x1_ready, 1)
                    if at(22):
                        dve.wait_ge(x1_ready, c * BLOCKS + BLOCKS)
                        dve.wait_ge(merged, c * 2 + 2)
                        dve.tensor_tensor(m2[:, own, :], m2[:, own, :], x[:, own, :], ALU.add).then_inc(base_ready, 1)
                if part == CONV:
                    for q in range(2):
                        if at(20):
                            dve.wait_ge(base_ready, CHUNKS)
                            dve.wait_ge(merge_done, c * 2 + (2 * CHUNKS + q + 1))
                            dve.tensor_tensor(v[:, 4 * q:4 * q + 4, :], tp[:, 2 + q, :].rearrange("p (b f) -> p b f", b=4),
                                              m2[:, bass.ds(c * BLOCKS + 4 * q, 4), :], ALU.add).then_inc(v_done, 1)
                    for q in range(2):
                        if at(21 + q):
                            v_stats(part, c, q)
                    if at(23):
                        v_mean_var(part, c)
                    if at(25):
                        inverse_std(part, c)
                        dve.scalar_tensor_tensor(shift[:, :], mean[:, :], -1.0, rstd[:, :], ALU.mult, ALU.mult)\
                           .then_inc(shift_done, 1)

            def tiles(k, prev):
                for j in range(TILES):
                    if prev:
                        tail(*prev, j)
                    if k.part == GCN:
                        branch2(k.c, j)
                    if k.peeled:
                        split_features(k, j)
                    if j not in k.whole:
                        split_tile(k, j)
                    if k.part == DEG:
                        sum_rows(k, j)
                    if k.part == GCN and k.peeled and j == 0:
                        dve.wait_ge(params_loaded, 16)
                        dve.tensor_scalar(scale[:, :], par[:, AT["eps1"]:AT["eps1"] + 2], 2.0, None, ALU.add)\
                           .then_inc(scale_ready, 1)

            schedule(dve, tiles, tail)

        @block.tensor
        def _(pe):
            def multiply(k, j):
                if j in k.whole:
                    pe.wait_ge(raw_loaded[j % RAW], k.loads(j))
                    if k.part == DEG:
                        pe.wait_ge(x2_loaded[j // BLOCKS], 16)
                        pe.wait_ge(rows_summed, k.sums_done(j))
                        plain = x2
                    else:
                        pe.wait_ge(x1_ready, j + 1)
                        plain = x
                else:
                    pe.wait_ge(lo_ready, k.splits_done(j))
                    if k.peeled:
                        pe.wait_ge(y_lo_ready, y_count(k.part, j))
                n = k.split.index(j) % SPL if j in k.split else None
                prior = before(k)
                sums = sum_banks(acc, k.part, k.c)
                for bank in range(BANKS[k.part]):
                    out = sums[:, bank, :]
                    cols = slice(bank % 2 * BANK, (bank % 2 + 1) * BANK)
                    first, last = j == 0, j == TILES - 1
                    if first and k.part != DEG and (k.peeled or k.part == GCN):
                        pe.wait_ge(bank_out, prior.banks + (bank % BANKS[prior.part] + 1))
                    if n is None:
                        mm = pe.matmul(out, plain[:, j, :], raw[:, j % RAW, cols], start=first, stop=last)
                    else:
                        y_hi, y_lo = ((y0_hi, y0_lo), (y1_hi, y1_lo))[bank // 2]
                        pe.matmul(out, y_hi[:, j, :], hi[:, n, cols], start=first, stop=False)
                        pe.matmul(out, y_lo[:, j, :], hi[:, n, cols], start=False, stop=False)
                        mm = pe.matmul(out, y_hi[:, j, :], lo[:, n, cols], start=False, stop=last)
                    if bank == BANKS[k.part] - 1:
                        mm.then_inc(tile_used, 1)
                    elif last:
                        mm.then_inc(bank_done, 1)

            def layer2(c, n_layer):
                weights = slice(n_layer * D, (n_layer + 1) * D)
                pe.wait_ge(w2_lo_ready, 1)
                if n_layer == 0 and not isinstance(c, int):
                    pe.wait_ge(u_done, c * BLOCKS)
                for n in range(2):
                    half = slice(n * BANK, (n + 1) * BANK)
                    pe.wait_ge(h_lo_ready, halves(GCN, c) + (2 * n_layer + n + 1))
                    pe.matmul(tp[:, n, :], w2_hi[:, weights], h_hi[:, half], start=True, stop=False)
                    pe.matmul(tp[:, n, :], w2_lo[:, weights], h_hi[:, half], start=False, stop=False)
                    pe.matmul(tp[:, n, :], w2_hi[:, weights], h_lo[:, half], start=False, stop=True).then_inc(layer_done, 1)

            def layer1(c, n_layer):
                src = (rows, h)[n_layer % 2]
                if n_layer == 0:
                    pe.wait_ge(u_done, CHUNKS * BLOCKS)
                for n in range(2):
                    if n_layer == 0:
                        pe.wait_ge(bank_out, Chunk(CONV, c, False).banks + (n + 1))
                    else:
                        pe.wait_ge(relu_done, halves(CONV, c) + (2 * n_layer - 2 + n + 1))
                    pe.matmul(tp[:, n, :], w("w1", n_layer), src[:, n * BANK:(n + 1) * BANK], start=True, stop=True)\
                      .then_inc(layer_done, 1)

            def merge(part, c):
                weights = w("wm2" if part == GCN else "wm1")
                for b in range(BLOCKS):
                    if b % 4 == 0:
                        pe.wait_ge(relu_done, halves(part, c) + (2 * LAYERS - 2 + b // 4 + 1))
                    mm = pe.matmul(tp[:, 2 + b // 4, b % 4 * D:(b % 4 + 1) * D], h[:, b * P:(b + 1) * P], weights,
                                   start=True, stop=True)
                    if b % 4 == 3:
                        mm.then_inc(merge_done, 1)

            def branch2(c, slot):
                for n in range(LAYERS):
                    if slot == LAYER_SLOTS[GCN][n]:
                        layer2(c, n)
                if slot == MERGE_SLOT[GCN]:
                    merge(GCN, c)

            def tail(part, c, slot):
                def at(n):
                    return slot is None or slot == n

                if part == DEG and at(0):
                    pe.wait_ge(ones_ready, 1)
                    pe.wait_ge(rows_summed, c * (TILES - 1) + (TILES - 1))
                    for b in range(BLOCKS):
                        mm = pe.matmul(deg_ps[:, b:b + 1], rows[:, b * P:(b + 1) * P], ones[:, :], start=True, stop=True)
                    mm.then_inc(deg_done, 1)
                if part == GCN:
                    if at(3):
                        pe.wait_ge(bank_out, c * BANKS[GCN] + (CHUNKS * BANKS[DEG] + BANKS[GCN]))
                        pe.wait_ge(params_loaded, 16)
                        pe.wait_ge(merged, c * 2 + 2)
                        for b in range(BLOCKS):
                            rows_of = slice(b % 4 * P, (b % 4 + 1) * P)
                            pe.matmul(pair_ps[:, b, 0:D], msg[:, b // 4, rows_of], w("w_f"), start=True, stop=True)
                            pe.matmul(pair_ps[:, b, D:2 * D], msg[:, 2 + b // 4, rows_of], w("w_s"),
                                      start=True, stop=True).then_inc(pair_done, 1)
                if part == CONV:
                    for n in range(LAYERS):
                        if at(LAYER_SLOTS[CONV][n]):
                            layer1(c, n)
                    if at(MERGE_SLOT[CONV]):
                        merge(part, c)

            def tiles(k, prev):
                for j in range(TILES):
                    if prev:
                        tail(*prev, j)
                    if k.part == GCN:
                        branch2(k.c, j)
                    multiply(k, j)

            schedule(pe, tiles, tail)


def kernel(**inputs):
    import concourse.bacc as bacc
    from concourse.bass_utils import run_bass_kernel_spmd

    def rep(a):
        return np.broadcast_to(np.asarray(a).reshape(1, -1), (P, np.asarray(a).size))

    def by_block(a):
        return np.ascontiguousarray(np.asarray(a).reshape(TILES, P, D).transpose(1, 0, 2))

    def layers(a):
        return np.asarray(a).transpose(2, 0, 1).reshape(D, LAYERS * D)

    adj = np.asarray(inputs["adj"])
    wm = np.asarray(inputs["L1_gnn_Wm"])
    arrays = {
        "adj_t": np.ascontiguousarray(adj.reshape(CHUNKS, CW, TILES, P).transpose(0, 2, 3, 1)),
        "x_t": by_block(inputs["x"]),
        "s_t": by_block(inputs["L0_gnn_spatial_x"]),
        "x2_t": by_block(inputs["L1_gnn_x2"]),
        "w2_t": np.ascontiguousarray(layers(inputs["L1_gnn_W2"])),
        "params": np.ascontiguousarray(np.concatenate([
            np.asarray(inputs["L0_gnn_W_f"]), np.asarray(inputs["L0_gnn_W_s"]),
            layers(inputs["L1_gnn_W1"]), wm[:, :D].T, wm[:, D:].T,
            rep(inputs["L0_gnn_b_f"]), rep(inputs["L0_gnn_b_s"]), rep(inputs["L0_gnn_W_att"]), rep(inputs["L1_gnn_bm"]),
            np.asarray(inputs["L1_gnn_b1"]).T, np.asarray(inputs["L1_gnn_b2"]).T,
            rep(inputs["L0_gnn_b_att"]), rep(inputs["L1_gnn_eps1"]), rep(inputs["L1_gnn_eps2"])], axis=1)),
    }
    nc = bacc.Bacc("TRN2", target_bir_lowering=False, num_devices=1)
    aps = [nc.dram_tensor(n, a.shape, mybir.dt.from_np(a.dtype), kind="ExternalInput").ap() for n, a in arrays.items()]
    out = nc.dram_tensor("out_t", (P, TILES, D), F32, kind="ExternalOutput").ap()
    build(nc, *aps, out)
    r = run_bass_kernel_spmd(nc, [arrays], core_ids=[0])
    got = r.results[0]["out_t"]
    return np.ascontiguousarray(np.asarray(got).transpose(1, 0, 2).reshape(N, D))
```

```python
from contextlib import ExitStack

import numpy as np

import concourse.bass as bass
from concourse import mybir

F32 = mybir.dt.float32
F32R = mybir.dt.float32r
ALU = mybir.AluOpType
ACT = mybir.ActivationFunctionType

P = 128
N = 4096
D = 128
TILES = N // P
CW = 1024
CHUNKS = N // CW
BLOCKS = CW // P
BANK = 512
RAW = 8
SPL = 4
LAYERS = 3
WARM_UP = 4
DEG_EPS = 1e-9
LN_EPS = 1e-5

DEG, GCN, CONV = range(3)
SETS = (1, 2, 1)
BANKS = tuple(s * CW // BANK for s in SETS)

WHOLE_DEG = tuple(j for j in range(2, TILES) if j % 3 != 1)
WHOLE_CONV0 = tuple(range(0, 24, 3))

X2_LOADS = (0, 4, 8, 16, 24, TILES)
X2_ISSUED = (None, None, 1, 8, 16)


def x2_load(j):
    return sum(j >= begin for begin in X2_LOADS[1:])


LAYER_SLOTS = {GCN: (11, 17, 23), CONV: (3, 7, 11)}
MERGE_SLOT = {GCN: 28, CONV: 14}

NORM_SHARE = (4, 4)

PARAMS = (("w_f", D), ("w_s", D), ("w1", LAYERS * D), ("wm1", D), ("wm2", D),
          ("b_fs", 2 * D), ("w_att", 2 * D), ("bm", D), ("b1", LAYERS), ("b2", LAYERS),
          ("b_att", 1), ("eps1", 1), ("eps2", 1))
AT, _at = {}, 0
for _name, _width in PARAMS:
    AT[_name] = _at
    _at += _width
PARAM_COLS = _at


def sum_banks(acc, part, c):
    return acc[:, :, :] if part == GCN else acc[:, bass.ds(c % 2 * 2, 2), :]


class Chunk:

    def __init__(self, part, c, peeled):
        self.part, self.c, self.peeled = part, c, peeled
        self.whole = WHOLE_DEG if part == DEG else WHOLE_CONV0 if part == CONV and peeled else ()
        self.split = [j for j in range(TILES) if j not in self.whole]
        self.first = part == DEG and peeled
        self.tiles = c * TILES + part * CHUNKS * TILES
        per_deg = TILES - len(WHOLE_DEG)
        if part == DEG:
            self.splits = c * per_deg
        elif part == GCN:
            self.splits = c * TILES + CHUNKS * per_deg
        elif peeled:
            self.splits = CHUNKS * (per_deg + TILES)
        else:
            self.splits = c * TILES + CHUNKS * (per_deg + TILES) - len(WHOLE_CONV0)
        self.banks = c * BANKS[part] + CHUNKS * sum(BANKS[:part])
        self.early_banks = c * (BANKS[part] - 1) + CHUNKS * sum(b - 1 for b in BANKS[:part])
        self.sums = c * (TILES - 2)

    def loads(self, j):
        c, before = self.c, self.part * CHUNKS * TILES // RAW
        return c * (16 * TILES // RAW) + 16 * (before + j // RAW + 1)

    def splits_done(self, j):
        return self.splits + (self.split.index(j) + 1)

    def sums_done(self, j):
        return self.sums + (j - 1 if j > 1 else j + 1)

    def tile_done(self, j):
        return self.tiles + (j + 1)


def before(k):
    if k.first:
        return None
    if k.peeled:
        return Chunk(k.part - 1, CHUNKS - 1, False)
    return Chunk(k.part, k.c - 1, False)


def schedule(engine, tiles, tail):
    for part in (DEG, GCN, CONV):
        tiles(Chunk(part, 0, True), None if part == DEG else (part - 1, CHUNKS - 1))
        with engine.Fori(1, CHUNKS) as c:
            tiles(Chunk(part, c, False), (part, c - 1))
    tail(CONV, CHUNKS - 1, None)


def build(nc, adj_t, x_t, s_t, x2_t, w2_t, params, out_t):
    with ExitStack() as st:
        def sb(name, shape, dt=F32):
            return st.enter_context(nc.sbuf_tensor(name, shape, dt))

        def sem(name):
            return st.enter_context(nc.semaphore(name))

        raw = sb("raw", [P, RAW, CW])
        hi = sb("hi", [P, SPL, CW], F32R)
        lo = sb("lo", [P, SPL, CW], F32R)
        x = sb("x", [P, TILES, D])
        x2 = sb("x2", [P, TILES, D])
        m2 = sb("m2", [P, TILES, D])
        y0_hi = sb("y0_hi", [P, TILES, D], F32R)
        y0_lo = sb("y0_lo", [P, TILES, D], F32R)
        y1_hi = sb("y1_hi", [P, TILES, D], F32R)
        y1_lo = sb("y1_lo", [P, TILES, D], F32R)
        par = sb("par", [P, PARAM_COLS])
        rows = sb("rows", [P, CW])
        h = sb("h", [P, CW])
        h_hi = sb("h_hi", [P, CW], F32R)
        h_lo = sb("h_lo", [P, CW], F32R)
        w2_hi = sb("w2_hi", [P, LAYERS * D], F32R)
        w2_lo = sb("w2_lo", [P, LAYERS * D], F32R)
        v = sb("v", [P, BLOCKS, D])
        row_total = v[:, :, :].rearrange("p b f -> p (b f)")
        ones = sb("ones", [P, 1])
        scale = sb("scale", [P, 2])
        deg = sb("deg", [P, BLOCKS])
        deg_root = sb("deg_root", [P, BLOCKS])
        d = sb("d", [P, TILES])
        logit = sb("logit", [P, BLOCKS])
        attn = sb("attn", [P, BLOCKS])
        stats = sb("stats", [P, BLOCKS, 6])
        pair = sb("pair", [P, 5, BLOCKS])
        mean = sb("mean", [P, BLOCKS])
        var = sb("var", [P, BLOCKS])
        std = sb("std", [P, BLOCKS])
        rstd = sb("rstd", [P, BLOCKS])
        shift = sb("shift", [P, BLOCKS])
        msg = x2[:, 0:2 * BLOCKS, :].rearrange("p (k b) f -> p k (b f)", k=4)
        u = x2[:, 2 * BLOCKS:4 * BLOCKS, :].rearrange("p (b k) f -> p b (k f)", k=2)

        def w(name, i=0, n=D):
            return par[:, AT[name] + i * D:AT[name] + i * D + n]

        def col(name, i=0):
            return par[:, AT[name] + i:AT[name] + i + 1]

        acc = st.enter_context(nc.psum_tensor("acc", [P, 4, BANK], F32))
        tp = st.enter_context(nc.psum_tensor("tp", [P, 4, BANK], F32))
        deg_ps = tp[:, 3, 0:BLOCKS]
        pair_ps = tp[:, :, :].rearrange("p k (b f) -> p (k b) f", b=2)

        raw_loaded = [sem(f"raw_loaded{i}") for i in range(RAW)]
        params_loaded = sem("params_loaded")
        x2_loaded = [sem(f"x2_loaded{i}") for i in range(len(X2_LOADS) - 1)]
        x_loaded = [sem(f"x_loaded{i}") for i in range(CHUNKS)]
        s_loaded = [sem(f"s_loaded{i}") for i in range(CHUNKS)]
        ones_ready = sem("ones_ready")
        zeros_ready = sem("zeros_ready")
        warm_up_done = sem("warm_up_done")
        scale_ready = sem("scale_ready")
        hi_ready = sem("hi_ready")
        lo_ready = sem("lo_ready")
        y_hi_ready = sem("y_hi_ready")
        y_lo_ready = sem("y_lo_ready")
        rows_summed = sem("rows_summed")
        tile_used = sem("tile_used")
        bank_done = sem("bank_done")
        bank_out = sem("bank_out")
        row_total_ready = sem("row_total_ready")
        deg_done = sem("deg_done")
        deg_ready = sem("deg_ready")
        deg_root_ready = sem("deg_root_ready")
        d_ready = sem("d_ready")
        w2_loaded = sem("w2_loaded")
        w2_hi_ready = sem("w2_hi_ready")
        w2_lo_ready = sem("w2_lo_ready")
        h_hi_ready = sem("h_hi_ready")
        h_lo_ready = sem("h_lo_ready")
        layer_done = sem("layer_done")
        relu_done = sem("relu_done")
        merge_done = sem("merge_done")
        merged = sem("merged")
        base_ready = sem("base_ready")
        pair_done = sem("pair_done")
        u_done = sem("u_done")
        gate_relu_done = sem("gate_relu_done")
        logit_done = sem("logit_done")
        diff_done = sem("diff_done")
        attn_done = sem("attn_done")
        mix_done = sem("mix_done")
        v_done = sem("v_done")
        stats_done = sem("stats_done")
        pair_summed = sem("pair_summed")
        var_parts_done = sem("var_parts_done")
        mean_done = sem("mean_done")
        var_done = sem("var_done")
        std_done = sem("std_done")
        rstd_done = sem("rstd_done")
        x1_ready = sem("x1_ready")
        shift_done = sem("shift_done")
        dve_norm_done = sem("dve_norm_done")
        act_norm_done = sem("act_norm_done")
        stored = sem("stored")
        last_stored = [sem(f"last_stored{i}") for i in range(2)]

        def y_count(part, j):
            if part == DEG:
                return sum(i not in WHOLE_DEG for i in range(j + 1))
            in_deg = TILES - len(WHOLE_DEG)
            return in_deg + 2 * (j + 1) if part == GCN else in_deg + 2 * TILES + j + 1

        def lns(part, c):
            return c + (CHUNKS if part == CONV else 0)

        def halves(part, c):
            return (c + (CHUNKS if part == CONV else 0)) * (2 * LAYERS)

        def split_slot_freed(eng, k, j):
            n = k.split.index(j)
            if n >= SPL:
                eng.wait_ge(tile_used, k.tile_done(k.split[n - SPL]))
            elif not k.first:
                b = before(k)
                eng.wait_ge(tile_used, b.tile_done(b.split[n - SPL]))

        def store(engine, c, share, done):
            count, offset = NORM_SHARE[share], share * NORM_SHARE[0]
            engine.wait_ge((dve_norm_done, act_norm_done)[share], c * count + count)
            engine.dma_start(out_t[:, bass.ds(c * BLOCKS + offset, count), :],
                             x2[:, bass.ds(c * BLOCKS + offset, count), :]).then_inc(done, 16)

        block = st.enter_context(nc.Block())

        @block.sync
        def _(sp):
            def tiles(k, prev):
                for j in range(TILES):
                    b, i = (k, j - RAW) if j >= RAW else (before(k), TILES + j - RAW)
                    if b is not None:
                        if i in b.whole:
                            sp.wait_ge(tile_used, b.tile_done(i))
                        elif b.part == DEG:
                            sp.wait_ge(rows_summed, b.sums_done(i))
                        else:
                            sp.wait_ge(lo_ready, b.splits_done(i))
                    sp.dma_start(raw[:, j % RAW, :], adj_t[k.c, j]).then_inc(raw_loaded[j % RAW], 16)

            schedule(sp, tiles, lambda part, c, slot: store(sp, c, 0, last_stored[0]))

        @block.gpsimd
        def _(pool):
            def split_features(part, j):
                src = x2 if part == DEG else x
                pool.wait_ge(y_hi_ready, y_count(part, j))
                pool.tensor_tensor(y0_lo[:, j, :], src[:, j, :], y0_hi[:, j, :].bitcast(F32), ALU.subtract)\
                    .then_inc(y_lo_ready, 1)

            for j in range(TILES):
                if j not in WHOLE_DEG:
                    split_features(DEG, j)
            pool.wait_ge(tile_used, TILES)
            pool.dma_start(par[:, :], params).then_inc(params_loaded, 16)
            for n in range(CHUNKS):
                pool.wait_ge(tile_used, TILES + (n + 2) * BLOCKS)
                own = slice(n * BLOCKS, (n + 1) * BLOCKS)
                pool.dma_start(x[:, own, :], x_t[:, own, :]).then_inc(x_loaded[n], 16)
            for n in range(CHUNKS):
                pool.wait_ge(tile_used, (CHUNKS - 1) * TILES + (n + 1) * BLOCKS)
                own = slice(n * BLOCKS, (n + 1) * BLOCKS)
                pool.dma_start(x2[:, own, :], s_t[:, own, :]).then_inc(s_loaded[n], 16)
            pool.wait_ge(row_total_ready, CHUNKS)
            pool.dma_start(h[:, 0:LAYERS * D], w2_t).then_inc(w2_loaded, 16)
            for j in range(TILES):
                split_features(CONV, j)
            with pool.Fori(0, CHUNKS - 1) as c:
                for share in range(2):
                    store(pool, c, share, stored)

        @block.scalar
        def _(act):
            def load_x2(n):
                own = slice(X2_LOADS[n], X2_LOADS[n + 1])
                act.dma_start(x2[:, own, :], x2_t[:, own, :]).then_inc(x2_loaded[n], 16)

            for n in range(len(X2_ISSUED)):
                if X2_ISSUED[n] is None:
                    load_x2(n)

            def split_tile(k, j):
                act.wait_ge(raw_loaded[j % RAW], k.loads(j))
                split_slot_freed(act, k, j)
                n = k.split.index(j) % SPL
                act.activation(hi[:, n, :], raw[:, j % RAW, :], ACT.Copy).then_inc(hi_ready, 1)

            def split_features(k, j):
                if k.part == DEG:
                    if j in k.whole:
                        return
                    act.wait_ge(x2_loaded[x2_load(j)], 16)
                    act.activation(y0_hi[:, j, :], x2[:, j, :], ACT.Copy).then_inc(y_hi_ready, 1)
                elif k.part == GCN:
                    act.wait_ge(tile_used, (CHUNKS - 1) * TILES + j + 1)
                    act.wait_ge(d_ready, j // BLOCKS + 1)
                    act.wait_ge(x_loaded[j // BLOCKS], 16)
                    act.activation(y0_hi[:, j, :], x[:, j, :], ACT.Copy, scale=d[:, j:j + 1]).then_inc(y_hi_ready, 1)
                    act.wait_ge(s_loaded[j // BLOCKS], 16)
                    act.activation(y1_hi[:, j, :], x2[:, j, :], ACT.Copy, scale=d[:, j:j + 1]).then_inc(y_hi_ready, 1)
                else:
                    act.wait_ge(tile_used, (2 * CHUNKS - 1) * TILES + j + 1)
                    act.wait_ge(x1_ready, j + 1)
                    act.activation(y0_hi[:, j, :], x[:, j, :], ACT.Copy).then_inc(y_hi_ready, 1)

            def copy_sums(part, c):
                k = Chunk(part, c, False)
                sums = sum_banks(acc, part, c)
                for n in range(BANKS[part]):
                    if n < BANKS[part] - 1:
                        act.wait_ge(bank_done, k.early_banks + (n + 1))
                    else:
                        act.wait_ge(tile_used, k.tile_done(TILES - 1))
                    if part == DEG:
                        dst = m2[:, bass.ds(c * BLOCKS + 4 * n, 4), :].rearrange("p b f -> p (b f)")
                    else:
                        dst = msg[:, n, :] if part == GCN else rows[:, n * BANK:(n + 1) * BANK]
                    act.activation(dst, sums[:, n, :], ACT.Copy).then_inc(bank_out, 1)

            def split_w2():
                act.wait_ge(w2_loaded, 16)
                act.activation(w2_hi[:, :], h[:, 0:LAYERS * D], ACT.Copy).then_inc(w2_hi_ready, 1)

            def split_ax2(c):
                for n in range(2):
                    act.activation(h_hi[:, n * BANK:(n + 1) * BANK], m2[:, bass.ds(c * BLOCKS + 4 * n, 4), :], ACT.Copy)\
                       .then_inc(h_hi_ready, 1)

            def relu_layer2(c, layer):
                by = scale[:, 1:2] if layer == 0 else 1.0
                if layer == 0:
                    act.wait_ge(scale_ready, 1)
                    act.wait_ge(w2_lo_ready, 1)
                for n in range(2):
                    half = slice(n * BANK, (n + 1) * BANK)
                    act.wait_ge(layer_done, halves(GCN, c) + (2 * layer + n + 1))
                    act.activation(h[:, half], tp[:, n, :], ACT.Relu, bias=col("b2", layer), scale=by).then_inc(relu_done, 1)
                    if layer < LAYERS - 1:
                        act.activation(h_hi[:, half], tp[:, n, :], ACT.Relu, bias=col("b2", layer), scale=by)\
                           .then_inc(h_hi_ready, 1)

            def branch2(k, slot):
                c = k.c
                if slot == 5:
                    if k.peeled:
                        split_w2()
                    split_ax2(c)
                for layer in range(LAYERS):
                    if slot == LAYER_SLOTS[GCN][layer] + 3:
                        relu_layer2(c, layer)

            def relu_layer1(c, layer):
                dst = (h, rows)[layer % 2]
                for n in range(2):
                    act.wait_ge(layer_done, halves(CONV, c) + (2 * layer + n + 1))
                    act.activation(dst[:, n * BANK:(n + 1) * BANK], tp[:, n, :], ACT.Relu, bias=col("b1", layer),
                                   scale=scale[:, 0:1] if layer == 0 else 1.0).then_inc(relu_done, 1)

            def root_var(part, c):
                act.wait_ge(var_done, lns(part, c) + 1)
                act.activation(std[:, :], var[:, :], ACT.Sqrt).then_inc(std_done, 1)

            def normalise(c, b):
                act.activation(x2[:, bass.ds(c * BLOCKS + b, 1), :], v[:, b:b + 1, :], ACT.Identity,
                               bias=shift[:, b:b + 1], scale=rstd[:, b:b + 1]).then_inc(act_norm_done, 1)

            def tail(part, c, slot):
                def at(n):
                    return slot is None or slot == n

                if at(2 if part == GCN else 3):
                    copy_sums(part, c)
                if part == GCN:
                    if at(9):
                        for q in range(2):
                            act.wait_ge(u_done, c * BLOCKS + 4 * (q + 1))
                            act.activation(u[:, 4 * q:4 * q + 4, :], u[:, 4 * q:4 * q + 4, :], ACT.Relu)\
                               .then_inc(gate_relu_done, 1)
                    if at(12):
                        act.wait_ge(logit_done, c * BLOCKS + BLOCKS)
                        act.activation(attn[:, :], logit[:, :], ACT.Sigmoid, bias=col("b_att")).then_inc(attn_done, 1)
                    if at(19):
                        root_var(part, c)
                    return
                if part == DEG and at(13):
                    act.wait_ge(deg_ready, c + 1)
                    act.activation(deg_root[:, :], deg[:, :], ACT.Sqrt).then_inc(deg_root_ready, 1)
                if part == CONV:
                    for layer in range(LAYERS):
                        if at(LAYER_SLOTS[CONV][layer] + 3):
                            relu_layer1(c, layer)
                    if at(26):
                        root_var(part, c)
                    for n in range(NORM_SHARE[1]):
                        if at(28 + n):
                            if n == 0:
                                act.wait_ge(shift_done, c + 1)
                            normalise(c, NORM_SHARE[0] + n)
                    if slot is None:
                        store(act, c, 1, last_stored[1])

            def tiles(k, prev):
                for j in range(TILES):
                    if prev:
                        tail(*prev, j)
                    if k.part == GCN:
                        branch2(k, j)
                    if k.first and j in X2_ISSUED:
                        load_x2(X2_ISSUED.index(j))
                    if k.peeled:
                        split_features(k, j)
                    if j not in k.whole:
                        split_tile(k, j)

            schedule(act, tiles, tail)
            act.wait_ge(stored, 2 * 16 * (CHUNKS - 1))
            for share in range(2):
                act.wait_ge(last_stored[share], 16)

        @block.vector
        def _(dve):
            dve.memset(ones[:, :], 1.0).then_inc(ones_ready, 1)
            dve.memset(rows[:, 0:BANK], 0.0).then_inc(zeros_ready, 1)

            def split_tile(k, j):
                dve.wait_ge(hi_ready, k.splits_done(j))
                split_slot_freed(dve, k, j)
                n = k.split.index(j) % SPL
                dve.tensor_tensor(lo[:, n, :], raw[:, j % RAW, :], hi[:, n, :].bitcast(F32), ALU.subtract)\
                   .then_inc(lo_ready, 1)

            def split_features(k, j):
                if k.part == GCN:
                    for n, (src, y_hi, y_lo) in enumerate(((x, y0_hi, y0_lo), (x2, y1_hi, y1_lo))):
                        dve.wait_ge(y_hi_ready, y_count(GCN, j) - 1 + n)
                        dve.scalar_tensor_tensor(y_lo[:, j, :], src[:, j, :], d[:, j:j + 1], y_hi[:, j, :].bitcast(F32),
                                                 ALU.mult, ALU.subtract).then_inc(y_lo_ready, 1)

            def sum_rows(k, j):
                if j < 2:
                    return
                sums = (rows, h)[j % 2]
                if j < 4:
                    dve.wait_ge(raw_loaded[j - 2], k.loads(j - 2))
                    if k.first:
                        dve.wait_ge(warm_up_done, 1)
                    else:
                        dve.wait_ge(row_total_ready, k.c)
                else:
                    dve.wait_ge(rows_summed, k.sums_done(j - 2))
                dve.wait_ge(raw_loaded[j % RAW], k.loads(j))
                first = raw[:, j - 2, :] if j < 4 else sums[:, :]
                dve.tensor_tensor(sums[:, :], first, raw[:, j % RAW, :], ALU.add).then_inc(rows_summed, 1)

            def split_w2():
                dve.wait_ge(w2_hi_ready, 1)
                dve.tensor_tensor(w2_lo[:, :], h[:, 0:LAYERS * D], w2_hi[:, :].bitcast(F32), ALU.subtract)\
                   .then_inc(w2_lo_ready, 1)

            def branch2(k, slot):
                c = k.c
                if slot == 5 and k.peeled:
                    split_w2()
                for layer in range(LAYERS):
                    if slot == (5, LAYER_SLOTS[GCN][0] + 4, LAYER_SLOTS[GCN][1] + 4)[layer]:
                        for n in range(2):
                            half = slice(n * BANK, (n + 1) * BANK)
                            src = h[:, half] if layer else m2[:, bass.ds(c * BLOCKS + 4 * n, 4), :]
                            dve.wait_ge(h_hi_ready, halves(GCN, c) + (2 * layer + n + 1))
                            dve.tensor_tensor(h_lo[:, half], src, h_hi[:, half].bitcast(F32), ALU.subtract)\
                               .then_inc(h_lo_ready, 1)
                if slot == TILES - 1:
                    bm = w("bm").rearrange("p (a f) -> p a f", a=1).to_broadcast([P, 4, D])
                    for q in range(2):
                        dve.wait_ge(merge_done, c * 2 + (q + 1))
                        dve.tensor_tensor(m2[:, bass.ds(c * BLOCKS + 4 * q, 4), :],
                                          tp[:, 2 + q, :].rearrange("p (b f) -> p b f", b=4), bm, ALU.add)\
                           .then_inc(merged, 1)

            def v_stats(part, c, begin, end):
                n = lns(part, c)
                dve.wait_ge(v_done, n * 2 + (begin // 4 + 1))
                for b in range(begin, end):
                    dve.bn_stats(stats[:, b, :], v[:, b, :]).then_inc(stats_done, 1)

            def pair_stats(part, c):
                n = lns(part, c)
                even, odd = stats[:, :, 0:3], stats[:, :, 3:6]
                dve.wait_ge(stats_done, n * BLOCKS + BLOCKS)
                dve.tensor_tensor(pair[:, 0, :], even[:, :, 1], odd[:, :, 1], ALU.add).then_inc(pair_summed, 1)
                dve.tensor_tensor(pair[:, 1, :], even[:, :, 1], odd[:, :, 1], ALU.subtract).then_inc(pair_summed, 1)
                dve.tensor_tensor(pair[:, 2, :], even[:, :, 2], odd[:, :, 2], ALU.add).then_inc(pair_summed, 1)

            def mean_and_parts(part, c):
                n = lns(part, c)
                dve.wait_ge(pair_summed, n * 3 + 3)
                dve.tensor_scalar(mean[:, :], pair[:, 0, :], 0.5, None, ALU.mult).then_inc(mean_done, 1)
                dve.scalar_tensor_tensor(pair[:, 3, :], pair[:, 1, :], 0.25, pair[:, 1, :], ALU.mult, ALU.mult)\
                   .then_inc(var_parts_done, 1)
                dve.tensor_scalar(pair[:, 4, :], pair[:, 2, :], 1.0 / D, LN_EPS, ALU.mult, ALU.add)\
                   .then_inc(var_parts_done, 1)

            def variance(part, c):
                n = lns(part, c)
                dve.wait_ge(var_parts_done, n * 2 + 2)
                dve.tensor_tensor(var[:, :], pair[:, 3, :], pair[:, 4, :], ALU.add).then_inc(var_done, 1)

            def inverse_std(part, c):
                dve.wait_ge(std_done, lns(part, c) + 1)
                dve.reciprocal(rstd[:, :], std[:, :]).then_inc(rstd_done, 1)
                dve.wait_ge(rstd_done, lns(part, c) + 1)

            def tail(part, c, slot):
                def at(n):
                    return slot is None or slot == n

                if part == DEG:
                    if at(1):
                        dve.wait_ge(rows_summed, c * (TILES - 2) + (TILES - 2))
                        dve.tensor_tensor(row_total[:, :], rows[:, :], h[:, :], ALU.add).then_inc(row_total_ready, 1)
                    if at(11):
                        dve.wait_ge(deg_done, c + 1)
                        dve.tensor_scalar(deg[:, :], deg_ps, DEG_EPS, None, ALU.add).then_inc(deg_ready, 1)
                    if at(14):
                        dve.wait_ge(deg_root_ready, c + 1)
                        dve.reciprocal(d[:, bass.ds(c * BLOCKS, BLOCKS)], deg_root[:, :]).then_inc(d_ready, 1)
                if part == GCN:
                    own = bass.ds(c * BLOCKS, BLOCKS)
                    for q in range(2):
                        if at(6 + q):
                            for b in range(4 * q, 4 * q + 4):
                                if b % 2 == 0:
                                    dve.wait_ge(pair_done, c * BLOCKS + (b + 2))
                                dve.scalar_tensor_tensor(u[:, b, :], pair_ps[:, b, :], d[:, bass.ds(c * BLOCKS + b, 1)],
                                                         w("b_fs", 0, 2 * D), ALU.mult, ALU.add).then_inc(u_done, 1)
                        if at(9 + q):
                            dve.wait_ge(gate_relu_done, c * 2 + (q + 1))
                            for b in range(4 * q, 4 * q + 4):
                                product = x2[:, 2 * b:2 * b + 2, :].rearrange("p k f -> p (k f)")
                                dve.tensor_tensor_reduce(product, u[:, b, :], w("w_att", 0, 2 * D), 1.0, 0.0,
                                                         ALU.mult, ALU.add, logit[:, b:b + 1]).then_inc(logit_done, 1)
                            half = slice(4 * q, 4 * q + 4)
                            dve.tensor_tensor(v[:, half, :], u[:, half, 0:D], u[:, half, D:2 * D], ALU.subtract)\
                               .then_inc(diff_done, 1)
                        if at(12 + q):
                            dve.wait_ge(attn_done, c + 1)
                            dve.wait_ge(diff_done, c * 2 + (q + 1))
                            for b in range(4 * q, 4 * q + 4):
                                dve.scalar_tensor_tensor(v[:, b, :], v[:, b, :], attn[:, b:b + 1], u[:, b, D:2 * D],
                                                         ALU.mult, ALU.add).then_inc(mix_done, 1)
                        if at(14):
                            dve.wait_ge(mix_done, c * BLOCKS + 4 * (q + 1))
                            half = slice(4 * q, 4 * q + 4)
                            dve.tensor_tensor(v[:, half, :], v[:, half, :], x[:, bass.ds(c * BLOCKS + 4 * q, 4), :],
                                              ALU.add).then_inc(v_done, 1)
                        if at(15 + q):
                            v_stats(part, c, 4 * q, 4 * q + 4)
                    if at(17):
                        pair_stats(part, c)
                        mean_and_parts(part, c)
                        variance(part, c)
                    if at(19):
                        inverse_std(part, c)
                    for q in range(2):
                        if at(20 + q):
                            for b in range(4 * q, 4 * q + 4):
                                dve.tensor_scalar(x[:, bass.ds(c * BLOCKS + b, 1), :], v[:, b:b + 1, :], mean[:, b:b + 1],
                                                  rstd[:, b:b + 1], ALU.subtract, ALU.mult).then_inc(x1_ready, 1)
                    if at(22):
                        dve.wait_ge(x1_ready, c * BLOCKS + BLOCKS)
                        dve.wait_ge(merged, c * 2 + 2)
                        dve.tensor_tensor(m2[:, own, :], m2[:, own, :], x[:, own, :], ALU.add).then_inc(base_ready, 1)
                if part == CONV:
                    for q in range(2):
                        if at(17 + 2 * q):
                            dve.wait_ge(base_ready, CHUNKS)
                            dve.wait_ge(merge_done, c * 2 + (2 * CHUNKS + q + 1))
                            dve.tensor_tensor(v[:, 4 * q:4 * q + 4, :], tp[:, 2 + q, :].rearrange("p (b f) -> p b f", b=4),
                                              m2[:, bass.ds(c * BLOCKS + 4 * q, 4), :], ALU.add).then_inc(v_done, 1)
                    for n in range(4):
                        if at(18 + n):
                            v_stats(part, c, 2 * n, 2 * n + 2)
                    if at(22):
                        pair_stats(part, c)
                    if at(23):
                        mean_and_parts(part, c)
                    if at(24):
                        variance(part, c)
                    if at(26):
                        inverse_std(part, c)
                        dve.scalar_tensor_tensor(shift[:, :], mean[:, :], -1.0, rstd[:, :], ALU.mult, ALU.mult)\
                           .then_inc(shift_done, 1)
                    for b in range(NORM_SHARE[0]):
                        if at(27 + b):
                            dve.tensor_scalar(x2[:, bass.ds(c * BLOCKS + b, 1), :], v[:, b:b + 1, :], mean[:, b:b + 1],
                                              rstd[:, b:b + 1], ALU.subtract, ALU.mult).then_inc(dve_norm_done, 1)

            def tiles(k, prev):
                for j in range(TILES):
                    if prev:
                        tail(*prev, j)
                    if k.part == GCN:
                        branch2(k, j)
                    if k.peeled:
                        split_features(k, j)
                    if j not in k.whole:
                        split_tile(k, j)
                    if k.part == DEG:
                        sum_rows(k, j)
                    if k.part == GCN and k.peeled and j == 0:
                        dve.wait_ge(params_loaded, 16)
                        dve.tensor_scalar(scale[:, :], par[:, AT["eps1"]:AT["eps1"] + 2], 2.0, None, ALU.add)\
                           .then_inc(scale_ready, 1)

            schedule(dve, tiles, tail)

        @block.tensor
        def _(pe):
            def multiply(k, j):
                if j in k.whole:
                    pe.wait_ge(raw_loaded[j % RAW], k.loads(j))
                    if k.part == DEG:
                        pe.wait_ge(x2_loaded[x2_load(j)], 16)
                        pe.wait_ge(rows_summed, k.sums_done(j))
                        plain = x2
                    else:
                        pe.wait_ge(x1_ready, j + 1)
                        plain = x
                else:
                    pe.wait_ge(lo_ready, k.splits_done(j))
                    if k.peeled:
                        pe.wait_ge(y_lo_ready, y_count(k.part, j))
                n = k.split.index(j) % SPL if j in k.split else None
                prior = before(k)
                sums = sum_banks(acc, k.part, k.c)
                for bank in range(BANKS[k.part]):
                    out = sums[:, bank, :]
                    cols = slice(bank % 2 * BANK, (bank % 2 + 1) * BANK)
                    first, last = j == 0, j == TILES - 1
                    if first and k.part != DEG and (k.peeled or k.part == GCN):
                        pe.wait_ge(bank_out, prior.banks + (bank % BANKS[prior.part] + 1))
                    if n is None:
                        mm = pe.matmul(out, plain[:, j, :], raw[:, j % RAW, cols], start=first, stop=last)
                    else:
                        y_hi, y_lo = ((y0_hi, y0_lo), (y1_hi, y1_lo))[bank // 2]
                        pe.matmul(out, y_hi[:, j, :], hi[:, n, cols], start=first, stop=False)
                        pe.matmul(out, y_lo[:, j, :], hi[:, n, cols], start=False, stop=False)
                        mm = pe.matmul(out, y_hi[:, j, :], lo[:, n, cols], start=False, stop=last)
                    if bank == BANKS[k.part] - 1:
                        mm.then_inc(tile_used, 1)
                    elif last:
                        mm.then_inc(bank_done, 1)

            def layer2(k, n_layer):
                c = k.c
                weights = slice(n_layer * D, (n_layer + 1) * D)
                pe.wait_ge(w2_lo_ready, 1)
                if n_layer == 0 and not k.peeled:
                    pe.wait_ge(u_done, c * BLOCKS)
                for n in range(2):
                    half = slice(n * BANK, (n + 1) * BANK)
                    pe.wait_ge(h_lo_ready, halves(GCN, c) + (2 * n_layer + n + 1))
                    pe.matmul(tp[:, n, :], w2_hi[:, weights], h_hi[:, half], start=True, stop=False)
                    pe.matmul(tp[:, n, :], w2_lo[:, weights], h_hi[:, half], start=False, stop=False)
                    pe.matmul(tp[:, n, :], w2_hi[:, weights], h_lo[:, half], start=False, stop=True).then_inc(layer_done, 1)

            def layer1(c, n_layer):
                src = (rows, h)[n_layer % 2]
                if n_layer == 0:
                    pe.wait_ge(u_done, CHUNKS * BLOCKS)
                for n in range(2):
                    if n_layer == 0:
                        pe.wait_ge(bank_out, Chunk(CONV, c, False).banks + (n + 1))
                    else:
                        pe.wait_ge(relu_done, halves(CONV, c) + (2 * n_layer - 2 + n + 1))
                    pe.matmul(tp[:, n, :], w("w1", n_layer), src[:, n * BANK:(n + 1) * BANK], start=True, stop=True)\
                      .then_inc(layer_done, 1)

            def merge(part, c):
                weights = w("wm2" if part == GCN else "wm1")
                for b in range(BLOCKS):
                    if b % 4 == 0:
                        pe.wait_ge(relu_done, halves(part, c) + (2 * LAYERS - 2 + b // 4 + 1))
                    mm = pe.matmul(tp[:, 2 + b // 4, b % 4 * D:(b % 4 + 1) * D], h[:, b * P:(b + 1) * P], weights,
                                   start=True, stop=True)
                    if b % 4 == 3:
                        mm.then_inc(merge_done, 1)

            def branch2(k, slot):
                for n in range(LAYERS):
                    if slot == LAYER_SLOTS[GCN][n]:
                        layer2(k, n)
                if slot == MERGE_SLOT[GCN]:
                    merge(GCN, k.c)

            def tail(part, c, slot):
                def at(n):
                    return slot is None or slot == n

                if part == DEG:
                    for b in range(BLOCKS):
                        if at(2 + b):
                            if b == 0:
                                pe.wait_ge(ones_ready, 1)
                                pe.wait_ge(row_total_ready, c + 1)
                            mm = pe.matmul(deg_ps[:, b:b + 1], row_total[:, b * P:(b + 1) * P], ones[:, :],
                                           start=True, stop=True)
                            if b == BLOCKS - 1:
                                mm.then_inc(deg_done, 1)
                if part == GCN:
                    if at(3):
                        pe.wait_ge(bank_out, c * BANKS[GCN] + (CHUNKS * BANKS[DEG] + BANKS[GCN]))
                        pe.wait_ge(params_loaded, 16)
                        pe.wait_ge(merged, c * 2 + 2)
                        for b in range(BLOCKS):
                            rows_of = slice(b % 4 * P, (b % 4 + 1) * P)
                            pe.matmul(pair_ps[:, b, 0:D], msg[:, b // 4, rows_of], w("w_f"), start=True, stop=True)
                            pe.matmul(pair_ps[:, b, D:2 * D], msg[:, 2 + b // 4, rows_of], w("w_s"),
                                      start=True, stop=True).then_inc(pair_done, 1)
                if part == CONV:
                    for n in range(LAYERS):
                        if at(LAYER_SLOTS[CONV][n]):
                            layer1(c, n)
                    if at(MERGE_SLOT[CONV]):
                        merge(part, c)

            def tiles(k, prev):
                for j in range(TILES):
                    if prev:
                        tail(*prev, j)
                    if k.part == GCN:
                        branch2(k, j)
                    multiply(k, j)

            pe.wait_ge(zeros_ready, 1)
            for n in range(WARM_UP):
                mm = pe.matmul(tp[:, 0, :], rows[:, 0:P], rows[:, 0:BANK], start=True, stop=True)
            mm.then_inc(warm_up_done, 1)
            schedule(pe, tiles, tail)


def kernel(**inputs):
    import concourse.bacc as bacc
    from concourse.bass_utils import run_bass_kernel_spmd

    def rep(a):
        return np.broadcast_to(np.asarray(a).reshape(1, -1), (P, np.asarray(a).size))

    def by_block(a):
        return np.ascontiguousarray(np.asarray(a).reshape(TILES, P, D).transpose(1, 0, 2))

    def layers(a):
        return np.asarray(a).transpose(2, 0, 1).reshape(D, LAYERS * D)

    adj = np.asarray(inputs["adj"])
    wm = np.asarray(inputs["L1_gnn_Wm"])
    arrays = {
        "adj_t": np.ascontiguousarray(adj.reshape(CHUNKS, CW, TILES, P).transpose(0, 2, 3, 1)),
        "x_t": by_block(inputs["x"]),
        "s_t": by_block(inputs["L0_gnn_spatial_x"]),
        "x2_t": by_block(inputs["L1_gnn_x2"]),
        "w2_t": np.ascontiguousarray(layers(inputs["L1_gnn_W2"])),
        "params": np.ascontiguousarray(np.concatenate([
            np.asarray(inputs["L0_gnn_W_f"]), np.asarray(inputs["L0_gnn_W_s"]),
            layers(inputs["L1_gnn_W1"]), wm[:, :D].T, wm[:, D:].T,
            rep(inputs["L0_gnn_b_f"]), rep(inputs["L0_gnn_b_s"]), rep(inputs["L0_gnn_W_att"]), rep(inputs["L1_gnn_bm"]),
            np.asarray(inputs["L1_gnn_b1"]).T, np.asarray(inputs["L1_gnn_b2"]).T,
            rep(inputs["L0_gnn_b_att"]), rep(inputs["L1_gnn_eps1"]), rep(inputs["L1_gnn_eps2"])], axis=1)),
    }
    nc = bacc.Bacc("TRN2", target_bir_lowering=False, num_devices=1)
    aps = [nc.dram_tensor(n, a.shape, mybir.dt.from_np(a.dtype), kind="ExternalInput").ap() for n, a in arrays.items()]
    out = nc.dram_tensor("out_t", (P, TILES, D), F32, kind="ExternalOutput").ap()
    build(nc, *aps, out)
    r = run_bass_kernel_spmd(nc, [arrays], core_ids=[0])
    got = r.results[0]["out_t"]
    return np.ascontiguousarray(np.asarray(got).transpose(1, 0, 2).reshape(N, D))
```
